# Optimizing a Trainium2 kernel written in Bass

```python
import numpy as np
import jax
import jax.numpy as jnp

def _softmax(x, axis=-1):
    return jax.nn.softmax(x, axis=axis)

def _gelu(x):
    return jax.nn.gelu(x, approximate=True)

def _silu(x):
    return jax.nn.silu(x)

def _sigmoid(x):
    return jax.nn.sigmoid(x)

def _layernorm(x, axis=-1, eps=1e-05):
    m = jnp.mean(x, axis=axis, keepdims=True)
    v = jnp.var(x, axis=axis, keepdims=True)
    return (x - m) / jnp.sqrt(v + eps)

def _scatter_add(tgt, idx, src, axis=0):
    return tgt.at[idx].add(src)

def _segment_sum(src, seg, n):
    return jax.ops.segment_sum(src, seg, n)
kernel_name = 'mk_seq_preln_d2_jaxref_r8_4d438c'

def setup_inputs(seed: int=0):
    np.random.seed(seed)
    _w = jnp.asarray

    def _L0_attn_setup():
        import jax, jax.numpy as jnp
        import numpy as np
        B, SQ, H = (2, 256, 256)
        NH = 16
        HN = H // NH
        key = jax.random.key(seed)
        ks = jax.random.split(key, 6)
        query = jax.random.normal(ks[0], (B, SQ, H), dtype=jnp.float32)
        k_in = jax.random.normal(ks[1], (B, SQ, H), dtype=jnp.float32)
        v_in = jax.random.normal(ks[2], (B, SQ, H), dtype=jnp.float32)
        Wqkv = jax.random.normal(ks[3], (3 * H, H), dtype=jnp.float32) * (1.0 / np.sqrt(H))
        Wproj = jax.random.normal(ks[4], (H, H), dtype=jnp.float32) * (1.0 / np.sqrt(H))
        bproj = jnp.zeros((H,), dtype=jnp.float32)
        return {'query': query, 'key': k_in, 'value': v_in, 'Wqkv': Wqkv, 'Wproj': Wproj, 'bproj': bproj}
    _L0_attn_in = _L0_attn_setup()

    def _L0_ffn_setup():
        import jax, jax.numpy as jnp
        import numpy as np
        B, T, D = (4, 128, 256)
        N, S, H = (8, 8, 8)
        ETA = 1.0
        key = jax.random.key(seed)
        ks = jax.random.split(key, 9)
        return {'x': jax.random.normal(ks[0], (B, T, D), jnp.float32), 'select_weight': jax.random.normal(ks[1], (N, D, S), jnp.float32) / D, 'select_mean_diff': jax.random.normal(ks[2], (N, D), jnp.float32) / D, 'imp_center': jax.random.normal(ks[3], (N,), jnp.float32), 'imp_slope': jax.random.normal(ks[4], (N,), jnp.float32) * 5.0, 'lora_update': jax.random.normal(ks[5], (N, D, H), jnp.float32) * 0.02, 'lora_degen': jax.random.normal(ks[6], (N, D, H), jnp.float32) * 0.02, 'bias_w': jax.random.normal(ks[7], (N, D), jnp.float32) * 0.02, 'debias_w': jax.random.normal(ks[8], (N, D), jnp.float32) * 0.02}
    _L0_ffn_in = _L0_ffn_setup()

    def _L1_attn_setup():
        import jax, jax.numpy as jnp
        import numpy as np
        B, S, E, H, G = (2, 256, 256, 16, 4)
        D = E // H
        key = jax.random.key(seed)
        ks = jax.random.split(key, 7)
        scale = 1.0 / np.sqrt(E)
        x = jax.random.normal(ks[0], (B, S, E), dtype=jnp.float32)
        Wq = jax.random.normal(ks[1], (H, E, D), dtype=jnp.float32) * scale
        bq = jax.random.normal(ks[2], (H, D), dtype=jnp.float32) * 0.02
        Wk = jax.random.normal(ks[3], (G, E, D), dtype=jnp.float32) * scale
        bk = jax.random.normal(ks[4], (G, D), dtype=jnp.float32) * 0.02
        Wv = jax.random.normal(ks[5], (G, E, D), dtype=jnp.float32) * scale
        bv = jax.random.normal(ks[6], (G, D), dtype=jnp.float32) * 0.02
        return {'x': x, 'Wq': Wq, 'bq': bq, 'Wk': Wk, 'bk': bk, 'Wv': Wv, 'bv': bv}
    _L1_attn_in = _L1_attn_setup()

    def _L1_ffn_setup():
        import jax, jax.numpy as jnp
        import numpy as np
        B, S, D = (2, 256, 256)
        I = 128
        E = 32
        K = 4
        NS = 1
        ALPHA = 7.0

        def _clamped_swiglu(x, wg, wu, wd):
            g = jnp.clip(x @ wg.T, -ALPHA, ALPHA)
            u = jnp.clip(x @ wu.T, -ALPHA, ALPHA)
            return jax.nn.silu(g) * u @ wd.T
        key = jax.random.key(seed)
        ks = jax.random.split(key, 9)
        s = 0.02
        return {'hidden': jax.random.normal(ks[0], (B, S, D), jnp.float32), 'router_w': jax.random.normal(ks[1], (E, D), jnp.float32) * s, 'expert_bias': jax.random.normal(ks[2], (E,), jnp.float32) * s, 'gate_w': jax.random.normal(ks[3], (E, I, D), jnp.float32) * s, 'up_w': jax.random.normal(ks[4], (E, I, D), jnp.float32) * s, 'down_w': jax.random.normal(ks[5], (E, D, I), jnp.float32) * s, 'shared_gate_w': jax.random.normal(ks[6], (NS * I, D), jnp.float32) * s, 'shared_up_w': jax.random.normal(ks[7], (NS * I, D), jnp.float32) * s, 'shared_down_w': jax.random.normal(ks[8], (D, NS * I), jnp.float32) * s}
    _L1_ffn_in = _L1_ffn_setup()
    _d = {'L0_attn_query': _L0_attn_in['query'], 'L0_attn_key': _L0_attn_in['key'], 'L0_attn_value': _L0_attn_in['value'], 'L0_attn_Wqkv': _L0_attn_in['Wqkv'], 'L0_attn_Wproj': _L0_attn_in['Wproj'], 'L0_attn_bproj': _L0_attn_in['bproj'], 'L0_ffn_select_weight': _L0_ffn_in['select_weight'], 'L0_ffn_select_mean_diff': _L0_ffn_in['select_mean_diff'], 'L0_ffn_imp_center': _L0_ffn_in['imp_center'], 'L0_ffn_imp_slope': _L0_ffn_in['imp_slope'], 'L0_ffn_lora_update': _L0_ffn_in['lora_update'], 'L0_ffn_lora_degen': _L0_ffn_in['lora_degen'], 'L0_ffn_bias_w': _L0_ffn_in['bias_w'], 'L0_ffn_debias_w': _L0_ffn_in['debias_w'], 'L1_attn_Wq': _L1_attn_in['Wq'], 'L1_attn_bq': _L1_attn_in['bq'], 'L1_attn_Wk': _L1_attn_in['Wk'], 'L1_attn_bk': _L1_attn_in['bk'], 'L1_attn_Wv': _L1_attn_in['Wv'], 'L1_attn_bv': _L1_attn_in['bv'], 'L1_ffn_router_w': _L1_ffn_in['router_w'], 'L1_ffn_expert_bias': _L1_ffn_in['expert_bias'], 'L1_ffn_gate_w': _L1_ffn_in['gate_w'], 'L1_ffn_up_w': _L1_ffn_in['up_w'], 'L1_ffn_down_w': _L1_ffn_in['down_w'], 'L1_ffn_shared_gate_w': _L1_ffn_in['shared_gate_w'], 'L1_ffn_shared_up_w': _L1_ffn_in['shared_up_w'], 'L1_ffn_shared_down_w': _L1_ffn_in['shared_down_w']}
    _x0 = _d['L0_attn_query']
    _d['L0_attn_query'] = jax.random.normal(jax.random.fold_in(jax.random.key(seed), 1), (8, 256, 256), dtype=_x0.dtype)
    del _x0
    return _d

def reference(L0_attn_query, L0_attn_key, L0_attn_value, L0_attn_Wqkv, L0_attn_Wproj, L0_attn_bproj, L0_ffn_select_weight, L0_ffn_select_mean_diff, L0_ffn_imp_center, L0_ffn_imp_slope, L0_ffn_lora_update, L0_ffn_lora_degen, L0_ffn_bias_w, L0_ffn_debias_w, L1_attn_Wq, L1_attn_bq, L1_attn_Wk, L1_attn_bk, L1_attn_Wv, L1_attn_bv, L1_ffn_router_w, L1_ffn_expert_bias, L1_ffn_gate_w, L1_ffn_up_w, L1_ffn_down_w, L1_ffn_shared_gate_w, L1_ffn_shared_up_w, L1_ffn_shared_down_w):

    def _L0_attn_ref(query, key, value, Wqkv, Wproj, bproj):
        import jax, jax.numpy as jnp
        import numpy as np
        B, SQ, H = (2, 256, 256)
        NH = 16
        HN = H // NH
        b, sq, h = query.shape
        nh, hn = (NH, HN)
        norm = 1.0 / jnp.sqrt(jnp.asarray(hn, query.dtype))
        x = jnp.transpose(query, (1, 0, 2)).reshape(sq * b, h)
        mixed = x @ Wqkv.T
        mixed = mixed.reshape(sq, b, nh, 3, hn)
        q = mixed[..., 0, :]
        k = mixed[..., 1, :]
        v = mixed[..., 2, :]
        q = q.reshape(sq, b * nh, hn).transpose(1, 0, 2)
        k = k.reshape(sq, b * nh, hn).transpose(1, 0, 2)
        v = v.reshape(sq, b * nh, hn).transpose(1, 0, 2)
        attn = jnp.einsum('gqd,gkd->gqk', q, k) * norm
        attn = jax.nn.softmax(attn, axis=-1)
        ctx = jnp.einsum('gqk,gkd->gqd', attn, v)
        ctx = ctx.reshape(nh, b, sq, hn)
        ctx = jnp.transpose(ctx, (2, 1, 0, 3)).reshape(sq * b, h)
        out = ctx @ Wproj.T + bproj
        out = out.reshape(sq, b, h)
        return jnp.transpose(out, (1, 0, 2))

    def _L0_ffn_ref(x, select_weight, select_mean_diff, imp_center, imp_slope, lora_update, lora_degen, bias_w, debias_w):
        import jax, jax.numpy as jnp
        import numpy as np
        B, T, D = (4, 128, 256)
        N, S, H = (8, 8, 8)
        ETA = 1.0
        x_diff = x[:, None, :, :] - select_mean_diff[None, :, None, :]
        x_diff = x_diff / jnp.linalg.norm(x_diff, axis=3, keepdims=True)
        cont = jnp.einsum('nds,bntd->bnts', select_weight, x_diff) ** 2
        score = cont.sum(axis=-1)
        gate = jax.nn.sigmoid(imp_slope[None, :, None] * (score - imp_center[None, :, None]))
        sel_scale = gate.max(axis=1)[..., None]
        sel_idx = gate.argmax(axis=1)
        debias = jnp.take(debias_w, sel_idx, axis=0)
        bias = jnp.take(bias_w, sel_idx, axis=0)
        upd = jnp.take(lora_update, sel_idx, axis=0)
        dgn = jnp.take(lora_degen, sel_idx, axis=0)
        x_debias = x - debias
        mod_x = jnp.einsum('btdh,btd->bth', upd, x_debias)
        degen_up = jnp.einsum('btdh,bth->btd', dgn, mod_x)
        mod_x_bias = ETA * (bias + degen_up)
        return (1.0 - sel_scale) * x + sel_scale * mod_x_bias

    def _L1_attn_ref(x, Wq, bq, Wk, bk, Wv, bv):
        import jax, jax.numpy as jnp
        import numpy as np
        B, S, E, H, G = (2, 256, 256, 16, 4)
        D = E // H
        h, e, d = Wq.shape
        g = Wk.shape[0]
        per = h // g
        s = x.shape[1]
        q = jnp.einsum('bse,hed->bhsd', x, Wq) + bq[None, :, None, :]
        kg = jnp.einsum('bse,ged->bgsd', x, Wk) + bk[None, :, None, :]
        vg = jnp.einsum('bse,ged->bgsd', x, Wv) + bv[None, :, None, :]
        k = jnp.repeat(kg, per, axis=1)
        v = jnp.repeat(vg, per, axis=1)
        scores = jnp.einsum('bhqd,bhkd->bhqk', q, k) * (1.0 / np.sqrt(d))
        causal = jnp.triu(jnp.ones((s, s), dtype=bool), k=1)
        scores = jnp.where(causal[None, None, :, :], -jnp.inf, scores)
        attn = jax.nn.softmax(scores, axis=-1)
        out = jnp.einsum('bhqk,bhkd->bhqd', attn, v)
        return out.transpose(0, 2, 1, 3).reshape(x.shape[0], s, h * d)

    def _L1_ffn_ref(hidden, router_w, expert_bias, gate_w, up_w, down_w, shared_gate_w, shared_up_w, shared_down_w):
        import jax, jax.numpy as jnp
        import numpy as np
        B, S, D = (2, 256, 256)
        I = 128
        E = 32
        K = 4
        NS = 1
        ALPHA = 7.0

        def _clamped_swiglu(x, wg, wu, wd):
            g = jnp.clip(x @ wg.T, -ALPHA, ALPHA)
            u = jnp.clip(x @ wu.T, -ALPHA, ALPHA)
            return jax.nn.silu(g) * u @ wd.T
        Bb, Ss, Dd = hidden.shape
        flat = hidden.reshape(-1, Dd)
        T = flat.shape[0]
        logits = flat @ router_w.T
        scores = jnp.sqrt(jax.nn.softplus(logits))
        _, idx = jax.lax.top_k(scores + expert_bias, K)
        topv = jnp.take_along_axis(scores, idx, axis=1)
        topv = topv / (topv.sum(axis=-1, keepdims=True) + 1e-20)
        probs = jnp.zeros((T, E), flat.dtype).at[jnp.arange(T)[:, None], idx].set(topv)

        def body(acc, xs):
            wg, wu, wd, p = xs
            return (acc + p[:, None] * _clamped_swiglu(flat, wg, wu, wd), None)
        out, _ = jax.lax.scan(body, jnp.zeros_like(flat), (gate_w, up_w, down_w, probs.T))
        out = out + _clamped_swiglu(flat, shared_gate_w, shared_up_w, shared_down_w)
        return out.reshape(Bb, Ss, Dd)
    x = L0_attn_query
    x = x + _L0_attn_ref(_layernorm(x, axis=-1), L0_attn_key, L0_attn_value, L0_attn_Wqkv, L0_attn_Wproj, L0_attn_bproj)
    x = x + _L0_ffn_ref(_layernorm(x, axis=-1), L0_ffn_select_weight, L0_ffn_select_mean_diff, L0_ffn_imp_center, L0_ffn_imp_slope, L0_ffn_lora_update, L0_ffn_lora_degen, L0_ffn_bias_w, L0_ffn_debias_w)
    x = x + _L1_attn_ref(_layernorm(x, axis=-1), L1_attn_Wq, L1_attn_bq, L1_attn_Wk, L1_attn_bk, L1_attn_Wv, L1_attn_bv)
    x = x + _L1_ffn_ref(_layernorm(x, axis=-1), L1_ffn_router_w, L1_ffn_expert_bias, L1_ffn_gate_w, L1_ffn_up_w, L1_ffn_down_w, L1_ffn_shared_gate_w, L1_ffn_shared_up_w, L1_ffn_shared_down_w)
    return x

_drawn_inputs = setup_inputs


def setup_inputs(seed=0):
    import zlib

    import numpy as np

    out = dict(_drawn_inputs(seed))
    spreads = {'L0_attn_bproj': (0.0, 0.1)}
    factors = {'L0_ffn_select_weight': 64.0,
     'L0_ffn_select_mean_diff': 64.0,
     'L0_ffn_lora_update': 3.077,
     'L0_ffn_lora_degen': 3.059,
     'L0_ffn_debias_w': 8.0,
     'L1_attn_bq': 8.0,
     'L1_attn_bk': 64.0,
     'L1_ffn_router_w': 8.0,
     'L1_ffn_expert_bias': 8.0,
     'L1_ffn_gate_w': 8.0,
     'L1_ffn_up_w': 8.0,
     'L1_ffn_down_w': 8.0,
     'L1_ffn_shared_gate_w': 5.02,
     'L1_ffn_shared_up_w': 4.974,
     'L1_ffn_shared_down_w': 4.952}
    for name, (base, spread) in spreads.items():
        noise = np.random.default_rng([zlib.crc32(name.encode()), seed]).standard_normal(out[name].shape)
        drawn = base * np.exp(spread * noise) if base else spread * noise
        out[name] = jnp.asarray(drawn.astype(out[name].dtype))
    for name, factor in factors.items():
        out[name] = (out[name] * factor).astype(out[name].dtype)
    return out
```

```python
from contextlib import ExitStack

import numpy as np
import concourse.bass as bass
from concourse import mybir

ALU = mybir.AluOpType
ACT = mybir.ActivationFunctionType
AX = mybir.AxisListType
F32 = mybir.dt.float32
BF16 = mybir.dt.bfloat16
I32 = mybir.dt.int32
U32 = mybir.dt.uint32

P = 128
SEQS, SEQ, D = 8, 256, 256
TOKENS = SEQS * SEQ
TILES = TOKENS // P
KD = D // P
HEADS, HD = 16, 16
GROUPS = 4
HALVES = 2
HT = TILES // HALVES
HS = SEQS // HALVES
HTOK = TOKENS // HALVES
CHUNK = 512
CHUNKS = HTOK // CHUNK
CT = CHUNK // P
QT = SEQ // P
VW = HD + 1
PARTS = 3
STACK = 6 * HD
ROWS = STACK + 2
Q_PARTS = (0, 0, 1, 1, 0, 2)
K_PARTS = (0, 1, 0, 1, 2, 0)
EPS = 1e-5
NSEL, SELW, LORA = 8, 8, 8
FW = NSEL * SELW + NSEL + NSEL * LORA
MW = NSEL * LORA + NSEL
EXPERTS, INNER, TOPK = 32, 128, 4
MASKED = -1.0e30
BLOCKS = -(-(TOKENS * TOPK + EXPERTS * (P - 1)) // P)
BLOCKS += BLOCKS % 2
EW = 2 * KD * INNER + D
CLAMP = 7.0
P_RING = 4
LAG = 3
JOB_BANKS = 6

JOBS0 = [(c, kind) for c in range(CHUNKS) for kind in ("T0", "T1", "Q0", "Q1", "K0", "K1", "V0", "V1")]
JOBS1 = [(c, kind) for c in range(CHUNKS) for kind in ("T0", "T1", "Q0", "Q1", "K0", "V0")]
SPLIT0 = [j for j in JOBS0 if j[1][0] in "QK"]
SPLIT1 = [j for j in JOBS1 if j[1][0] in "QK"]
FFN_JOBS = 2 * CHUNKS + HT // 2 + CHUNKS + HT // 2
JOB_F = 2 * CHUNKS + HT // 2
JOB_1 = JOB_F + FFN_JOBS

UNITS = (
    [(qt, h, 2, SEQ) for h in range(0, HEADS, 2) for qt in range(QT)],
    [(0, h, 4, P) for h in range(0, HEADS, 4)] + [(1, h, 2, SEQ) for h in range(0, HEADS, 2)],
)
DVE_STEPS = (11,28)


def heads_of_kv(layer, h):
    return h if layer == 0 else h // (HEADS // GROUPS)


def two_block_kernel(nc, x_in, wqkv0, wproj, bproj, wffn, debias, wdown, center, slope,
                     wqkv1, bq1, bk1, bv1, router, ebias, wexp_in, out):
    ctx = ExitStack()
    with ctx:
        def sb(name, shape, dt=F32):
            return ctx.enter_context(nc.sbuf_tensor(name, shape, dt))

        def sem(name):
            return ctx.enter_context(nc.semaphore(name))

        def cut(whole, start, size, shape=None, **axes):
            part = whole[:, start:start + size]
            return part.rearrange(shape, **axes) if shape else part

        x = sb("x", [P, TILES, D])
        norms = sb("norms", [P, TILES * D])
        xn = cut(norms, 0, HT * D, "p (t d) -> p t d", t=HT)
        xnT = cut(norms, HT * D, KD * HTOK, "p (k t) -> p k t", k=KD)
        xnT4 = cut(norms, 0, KD * TOKENS, "p (k t) -> p k t", k=KD)
        attn_w = sb("attn_w", [P, KD * (3 * D + D + D + 2 * GROUPS * HD)])
        w0 = cut(attn_w, 0, KD * 3 * D, "p (k n) -> p k n", k=KD)
        wp = cut(attn_w, KD * 3 * D, KD * D, "p (k n) -> p k n", k=KD)
        w1 = cut(attn_w, KD * 4 * D, KD * (D + 2 * GROUPS * HD), "p (k n) -> p k n", k=KD)
        xb = cut(attn_w, 0, 2 * D, "p (b d) -> p b d", b=2)
        xbT = cut(attn_w, 2 * D, 2 * D, "p (b k t) -> p b k t", b=2, k=KD)
        gu = cut(attn_w, 4 * D, 4 * INNER, "p (b g i) -> p b g i", b=2, g=2)
        ge = cut(attn_w, 6 * D, 2 * INNER, "p (b i) -> p b i", b=2)
        hid = cut(attn_w, 6 * D + 2 * INNER, 2 * INNER, "p (b i) -> p b i", b=2)
        hidT = cut(attn_w, 6 * D + 4 * INNER, 2 * P, "p (b t) -> p b t", b=2)
        yb = cut(attn_w, 6 * D + 6 * INNER, 2 * D, "p (b d) -> p b d", b=2)
        ffn_w = sb("ffn_w", [P, KD * FW])
        wf = cut(ffn_w, 0, KD * FW, "p (k f) -> p k f", k=KD)
        wdb = sb("wdb", [P, KD, NSEL])
        wd_all = sb("wd", [P, D])
        wd = wd_all[0:MW, :]
        bpb = sb("bpb", [P, D])
        bq = sb("bq", [P, KD])
        bk = sb("bk", [GROUPS * HD, 1])
        bvb = sb("bvb", [P, GROUPS * HD])
        cenb = sb("cenb", [P, NSEL])
        slob = sb("slob", [P, NSEL])
        ident = sb("ident", [P, P])
        identb = sb("identb", [P, P], BF16)
        ones = sb("ones", [P, P])
        mask_s = sb("mask_s", [P, P], BF16)
        mask_t = sb("mask_t", [P, P], BF16)
        iota8 = sb("iota8", [P, NSEL])
        products = sb("products", [P, KD * FW])
        prod = cut(products, 0, KD * FW, "p (k f) -> p k f", k=KD)
        constb = sb("constb", [P, FW])
        sizes = [HEADS * HTOK // 2, HT * HEADS * VW, SEQS * QT * HEADS * HD, HEADS * HTOK // 2,
                 GROUPS * HTOK // 2, HT * GROUPS * VW]
        at = [sum(sizes[:i]) for i in range(len(sizes) + 1)]
        arena = sb("arena", [P, max(at[-1], EXPERTS * EW)])
        stack = "p (h t) -> p h t"
        ks = [cut(arena, at[0], sizes[0]).bitcast(BF16).rearrange(stack, h=HEADS)[0:ROWS],
              cut(arena, at[4], sizes[4]).bitcast(BF16).rearrange(stack, h=GROUPS)[0:ROWS]]
        qs = cut(arena, at[3], sizes[3]).bitcast(BF16).rearrange(stack, h=HEADS)[0:ROWS]
        v = [cut(arena, at[1], sizes[1], "p (t h w) -> p t h w", t=HT, h=HEADS),
             cut(arena, at[5], sizes[5], "p (t h w) -> p t h w", t=HT, h=GROUPS)]
        splits = sb("splits", [P, 4 * PARTS * CHUNK // 2 + 4 * CHUNK])
        parts = cut(splits, 0, 4 * PARTS * CHUNK // 2).bitcast(BF16).rearrange(
            "p (s a t) -> p s a t", s=4, a=PARTS)
        rest = cut(splits, 4 * PARTS * CHUNK // 2, 4 * CHUNK, "p (s t) -> p s t", s=4)
        xn4 = cut(splits, 0, TILES * D, "p (t d) -> p t d", t=TILES)
        te = TILES * EXPERTS
        tile_expert = "p (t e) -> p t e"
        lg = cut(splits, TILES * D, te, tile_expert, t=TILES)
        sp1 = cut(splits, TILES * D + te, te, tile_expert, t=TILES)
        exps = sb("exps", [P, P_RING * 2 * SEQ])
        pt = cut(exps, 0, P_RING * 2 * SEQ, "p (r t) -> p r t", r=P_RING)
        work = cut(exps, 0, TILES * TOPK * EXPERTS, "p (t k e) -> p t k e", t=TILES, k=TOPK)
        pick = sb("pick", [P, TILES, TOPK, EXPERTS])
        mx = sb("mx", [P, QT, HEADS])
        neg = sb("neg", [P, QT, 2, HEADS], BF16)
        negT = sb("negT", [2 * HEADS, SEQ], BF16)
        rec = sb("rec", [P, QT, HEADS])
        rowbuf = sb("rowbuf", [P, QT * D + HT * FW + HT * NSEL * SELW + HT * MW])
        att = cut(rowbuf, 0, QT * D, "p (q d) -> p q d", q=QT)
        ctx0 = cut(arena, at[2], sizes[2], "p (j q h d) -> p j q h d", j=SEQS, q=QT, h=HEADS)
        st = sb("st", [P, TILES, 6])
        mv = sb("mv", [P, TILES, 2])
        var = sb("var", [P, TILES])
        sd = sb("sd", [P, TILES])
        rstd = sb("rstd", [P, TILES])
        g = cut(rowbuf, QT * D, HT * FW, "p (t f) -> p t f", t=HT)
        sq = cut(rowbuf, QT * D + HT * FW, HT * NSEL * SELW, "p (t f) -> p t f", t=HT)
        xx = sb("xx", [P, HT])
        sc = [sb(f"sc{i}", [P, HT, NSEL]) for i in range(4)]
        top = sb("top", [P, HT])
        least = sb("least", [P, HT])
        keep = sb("keep", [P, HT])
        mm = cut(rowbuf, QT * D + HT * FW + HT * NSEL * SELW, HT * MW, "p (t f) -> p t f", t=HT)
        sg, su, se, sh = (cut(rowbuf, i * CHUNK, CHUNK) for i in range(4))
        slots_e = cut(rowbuf, 4 * CHUNK, te, tile_expert, t=TILES)
        turned_m = sb("turned_m", [P, HTOK])
        mT = turned_m[0:MW, :]
        sco = cut(turned_m, 0, te, tile_expert, t=TILES)
        sbi = cut(turned_m, te, te, tile_expert, t=TILES)
        wr = sb("wr", [P, KD, EXPERTS])
        wsh = sb("wsh", [P, EW])
        ebb = sb("ebb", [P, EXPERTS])
        iota32 = sb("iota32", [P, EXPERTS])
        iota_b = sb("iota_b", [1, BLOCKS])
        zero = sb("zero", [P, 64])
        before = sb("before", [P, P], BF16)
        onesb = sb("onesb", [P, P], BF16)
        m8 = cut(ffn_w, 0, TILES * 8, "p (t e) -> p t e", t=TILES)
        i8 = cut(ffn_w, TILES * 8, TILES * 8).bitcast(U32).rearrange("p (t e) -> p t e", t=TILES)
        pk = [sb(f"pk{i}", [P, TILES, TOPK]) for i in range(2)]
        ps = [sb(f"ps{i}", [P, TILES]) for i in range(2)]
        chosen = cut(products, 0, te // 2).bitcast(BF16).rearrange(tile_expert, t=TILES)
        cnt = [cut(wd_all, i * EXPERTS, EXPERTS) for i in range(4)]
        eb_f = wd_all[0:1, 4 * EXPERTS:4 * EXPERTS + BLOCKS]
        cnti = [cut(bpb, i * EXPERTS, EXPERTS).bitcast(I32) for i in range(2)]
        slot = cut(bpb, 2 * EXPERTS, TILES * TOPK).bitcast(U32).rearrange("p (t k) -> p t k", t=TILES)
        eb_i = sb("eb_i", [1, BLOCKS], I32)
        YG = 8
        yg = cut(arena, 0, YG * D, "p (r d) -> p r d", r=YG)

        bank = [ctx.enter_context(nc.psum_tensor(f"bank{i}", [P, 512], F32)) for i in range(8)]
        unit_bank, st_bank, pv_bank, misc = bank[0:2], bank[2:5], bank[5:7], bank[7]

        scratch = [nc.dram_tensor(f"parts_dram{n}", [CHUNKS, PARTS, c, CHUNK], BF16, kind="Internal").ap()
                   for n, c in ((0, 2 * D), (1, D + GROUPS * HD))]
        xs = nc.dram_tensor("rows_by_expert", [BLOCKS * P, D], F32, kind="Internal").ap()
        ys = nc.dram_tensor("results_by_expert", [BLOCKS * P, D], F32, kind="Internal").ap()

        weights_loaded = sem("weights_loaded")
        x_loaded = sem("x_loaded")
        constants_made = sem("constants_made")
        pool_step = sem("pool_step")
        products_made = sem("products_made")
        sums_made = sem("sums_made")
        sums_copied = sem("sums_copied")
        dve_step = [sem(f"dve_step{n}") for n in range(2)]
        act_step = sem("act_step")
        var_ready = [sem(f"var_ready{n}") for n in range(2)]
        sd_ready = [sem(f"sd_ready{n}") for n in range(2)]
        xn_ready = [sem(f"xn_ready{n}") for n in range(2)]
        bias_added = sem("bias_added")
        rows_moved = sem("rows_moved")
        job_ready = [sem(f"job_ready{n}") for n in range(2)]
        job_done = [sem(f"job_done{n}") for n in range(2)]
        hi_ready = [sem(f"hi_ready{n}") for n in range(2)]
        mid_ready = [sem(f"mid_ready{n}") for n in range(2)]
        low_ready = [sem(f"low_ready{n}") for n in range(2)]
        saved = [[sem(f"saved{n}_{i}") for i in range(4)] for n in range(2)]
        stacked = [[sem(f"stacked{n}_{c}") for c in range(CHUNKS)] for n in range(2)]
        unit_ready = [sem(f"unit_ready{n}") for n in range(2)]
        unit_done = [sem(f"unit_done{n}") for n in range(2)]
        neg_ready = [sem(f"neg_ready{n}") for n in range(2)]
        negT_ready = [sem(f"negT_ready{n}") for n in range(2)]
        negT_copied = [sem(f"negT_copied{n}") for n in range(2)]
        neg_stacked = [sem(f"neg_stacked{n}") for n in range(2)]
        st_ready = [sem(f"st_ready{n}") for n in range(2)]
        exp_ready = [sem(f"exp_ready{n}") for n in range(2)]
        pv_ready = [sem(f"pv_ready{n}") for n in range(2)]
        att_ready = [sem(f"att_ready{n}") for n in range(2)]
        squares_ready = sem("squares_ready")
        logit_ready = sem("logit_ready")
        gate_exp_ready = sem("gate_exp_ready")
        selected = sem("selected")
        out_done = sem("out_done")
        xs_cleared = sem("xs_cleared")
        experts_loaded = sem("experts_loaded")
        xn4_ready = sem("xn4_ready")
        var4_ready = sem("var4_ready")
        sd4_ready = sem("sd4_ready")
        turn4_ready = sem("turn4_ready")
        turn4_copied = sem("turn4_copied")
        logits_ready = sem("logits_ready")
        route_ready = sem("route_ready")
        route_act = sem("route_act")
        chosen_ready = sem("chosen_ready")
        ranks_ready = sem("ranks_ready")
        slots_ready = sem("slots_ready")
        blocks_ready = sem("blocks_ready")
        scattered = sem("scattered")
        moe_step = sem("moe_step")
        sgu_ready = sem("sgu_ready")
        sgu_clipped = sem("sgu_clipped")
        sexp_ready = sem("sexp_ready")
        shid_ready = sem("shid_ready")
        sdown_ready = sem("sdown_ready")
        sdown_added = sem("sdown_added")
        xb_loaded = [sem(f"xb_loaded{i}") for i in range(2)]
        xb_turned = sem("xb_turned")
        xbT_copied = sem("xbT_copied")
        gu_ready = sem("gu_ready")
        gu_clipped = sem("gu_clipped")
        ge_ready = sem("ge_ready")
        hid_step = sem("hid_step")
        hid_ready = sem("hid_ready")
        hid_turned = sem("hid_turned")
        hidT_copied = sem("hidT_copied")
        y_ready = sem("y_ready")
        yb_copied = sem("yb_copied")
        y_stored = [sem(f"y_stored{i}") for i in range(2)]
        gathered = [sem(f"gathered{i}") for i in range(8)]
        y_added = sem("y_added")

        RING = (4, 3)
        SPLITS = (SPLIT0, SPLIT1)
        LAYER_JOBS = (JOBS0, JOBS1)
        JOB0 = (0, JOB_1)
        JOBS = (len(JOBS0), JOB_1 + len(JOBS1))
        NORMS = (1, 2)
        QK_ROWS = (2 * D, D + GROUPS * HD)

        def pair_of(b, p):
            return b // 2 if isinstance(b, int) else (b - p) // 2

        def wide(row, n):
            return row.broadcast_to([P, n])

        def halves(w):
            return w.rearrange("(k p) n -> p k n", p=P)

        CONSTANTS = 13
        WEIGHTS = [
            (wf[:, :, :], halves(wffn)), (wdb[:, :, :], halves(debias)), (w0[:, :, :], halves(wqkv0)),
            (wp[:, :, :], halves(wproj)), (wd, wdown), (bpb[:, :], wide(bproj, D)),
            (cenb[:, :], wide(center, NSEL)), (slob[:, :], wide(slope, NSEL)),
            (wr[:, :, :], halves(router)), (ebb[:, :], wide(ebias, EXPERTS)), (wsh[:, :], wexp_in[:, EXPERTS, :]),
            (w1[:, :, :], halves(wqkv1)), (bq[:, :], bq1), (bk[:, :], bk1), (bvb[:, :], wide(bv1, GROUPS * HD)),
        ]

        block = ctx.enter_context(nc.Block())

        @block.sync
        def _(sp):
            xr = x_in.rearrange("(t p) d -> p t d", p=P)
            sp.dma_start(x[:, 0:HT, :], xr[:, 0:HT, :]).then_inc(x_loaded, 16)
            for dst, src in WEIGHTS:
                sp.dma_start(dst, src).then_inc(weights_loaded, 16)
            sp.wait_ge(x_loaded, 16)
            sp.dma_start(x[:, HT:TILES, :], xr[:, HT:TILES, :]).then_inc(x_loaded, 16)

            sp.wait_ge(constants_made, CONSTANTS)
            sp.dma_start(xs.rearrange("(p r) (a c) -> p (r a) c", p=P, c=64),
                         zero[:, :].unsqueeze(1).broadcast_to([P, BLOCKS * D // 64, 64])).then_inc(xs_cleared, 16)

            def restack(half, n):
                kv = HEADS if n == 0 else GROUPS
                per_chunk = len(SPLITS[n]) // CHUNKS
                for c in range(CHUNKS):
                    for i in range(per_chunk):
                        j = c * per_chunk + i
                        slot = j % RING[n]
                        rows = min(P, QK_ROWS[n] - i * P)
                        sp.wait_ge(low_ready[n], half * len(SPLITS[n]) + j + 1)
                        sp.dma_start(scratch[n][c, :, i * P:i * P + rows, :].rearrange("a r t -> r a t"),
                                     parts[0:rows, slot, :, :]).then_inc(saved[n][slot], 16)
                    for slot in range(RING[n]):
                        uses = len([j for j in range(len(SPLITS[n])) if j % RING[n] == slot])
                        upto = len([j for j in range((c + 1) * per_chunk) if j % RING[n] == slot])
                        sp.wait_ge(saved[n][slot], (half * uses + upto) * 16)
                    at = slice(c * CHUNK, (c + 1) * CHUNK)
                    for blk in range(6):
                        rows = slice(blk * HD, (blk + 1) * HD)
                        sp.dma_start(qs[rows, :, at],
                                     scratch[n][c, Q_PARTS[blk], 0:D, :].rearrange("(h d) t -> d h t", d=HD)
                                     ).then_inc(stacked[n][c], 16)
                        sp.dma_start(ks[n][rows, :, at],
                                     scratch[n][c, K_PARTS[blk], D:D + kv * HD, :]
                                     .rearrange("(h d) t -> d h t", d=HD)).then_inc(stacked[n][c], 16)

            def stack_maxima(half, n):
                for b in range(HS):
                    sp.wait_ge(negT_copied[n], half * HS + b + 1)
                    for part in range(2):
                        sp.dma_start(qs[STACK + part:STACK + part + 1, :, b * SEQ:(b + 1) * SEQ],
                                     negT[part * HEADS:(part + 1) * HEADS, :]).then_inc(neg_stacked[n], 16)

            for half in range(HALVES):
                restack(half, 0)
                stack_maxima(half, 0)
            for half in range(HALVES):
                restack(half, 1)
                stack_maxima(half, 1)
            sp.wait_ge(att_ready[1], SEQS)
            sp.dma_start(arena[:, 0:EXPERTS * EW].rearrange("p (e w) -> p e w", e=EXPERTS),
                         wexp_in[:, 0:EXPERTS, :]).then_inc(experts_loaded, 16)
            sp.wait_ge(scattered, TILES * TOPK * 16)

            def load_block(b, p, again):
                if again:
                    sp.wait_ge(xb_turned, b - 1)
                sp.dma_start(xb[:, p, :], xs[bass.ds(b * P, P), :]).then_inc(xb_loaded[p], 16)

            load_block(0, 0, False)
            load_block(1, 1, False)
            with sp.Fori(1, BLOCKS // 2) as i:
                load_block(2 * i, 0, True)
                load_block(2 * i + 1, 1, True)
            outr = out.rearrange("(t p) d -> p t d", p=P)
            for t in range(0, TILES, 2):
                sp.wait_ge(y_added, (t + 2) * TOPK)
                sp.dma_start(outr[:, t:t + 2, :], x[:, t:t + 2, :]).then_inc(out_done, 16)
            sp.wait_ge(out_done, TILES // 2 * 16)

        @block.gpsimd
        def _(pool):
            pool.memset(ident[:, :], 0.0).then_inc(pool_step, 1)
            pool.memset(mask_s[:, :], 0.0).then_inc(pool_step, 1)
            pool.memset(mask_t[:, :], 0.0).then_inc(pool_step, 1)
            pool.memset(before[:, :], 1.0).then_inc(pool_step, 1)
            pool.memset(onesb[:, :], 1.0).then_inc(constants_made, 1)
            pool.memset(zero[:, :], 0.0).then_inc(constants_made, 1)
            pool.iota(iota32[:, :], [[1, EXPERTS]], base=0, channel_multiplier=0,
                      allow_small_or_imprecise_dtypes=True).then_inc(constants_made, 1)
            pool.memset(ones[:, :], 1.0).then_inc(constants_made, 1)
            for n in range(2):
                pool.memset(v[n][:, :, :, HD:VW], 1.0).then_inc(constants_made, 1)
            pool.iota(iota8[:, :], [[1, NSEL]], base=0, channel_multiplier=0,
                      allow_small_or_imprecise_dtypes=True).then_inc(constants_made, 1)
            pool.wait_ge(pool_step, 4)
            pool.affine_select(out=ident[:, :], in_=ident[:, :], compare_op=ALU.not_equal, fill=1.0, base=0,
                               pattern=[[-1, P]], channel_multiplier=1).then_inc(pool_step, 1)
            pool.affine_select(out=mask_s[:, :], in_=mask_s[:, :], compare_op=ALU.is_ge, fill=MASKED, base=0,
                               pattern=[[-1, P]], channel_multiplier=1).then_inc(constants_made, 1)
            pool.affine_select(out=mask_t[:, :], in_=mask_t[:, :], compare_op=ALU.is_ge, fill=MASKED, base=0,
                               pattern=[[1, P]], channel_multiplier=-1).then_inc(constants_made, 1)
            pool.affine_select(out=before[:, :], in_=before[:, :], compare_op=ALU.is_gt, fill=0.0, base=0,
                               pattern=[[1, P]], channel_multiplier=-1).then_inc(constants_made, 1)
            pool.wait_ge(pool_step, 5)
            pool.tensor_copy(identb[:, :], ident[:, :]).then_inc(constants_made, 1)

            def low_parts(half, n):
                for j, (c, kind) in enumerate(SPLITS[n]):
                    rows = GROUPS * HD if n == 1 and kind == "K0" else P
                    slot = j % RING[n]
                    pool.wait_ge(mid_ready[n], half * len(SPLITS[n]) + j + 1)
                    if rows < P:
                        pool.wait_ge(low_ready[n], half * len(SPLITS[n]) + j)
                    pool.tensor_tensor(parts[0:rows, slot, 2, :], rest[0:rows, slot, :],
                                       parts[0:rows, slot, 1, :], ALU.subtract).then_inc(low_ready[n], 1)

            for half in range(HALVES):
                low_parts(half, 0)
                pool.wait_ge(weights_loaded, 16 * len(WEIGHTS))
                pool.wait_ge(xn_ready[0], (half + 1) * HT)
                pool.tensor_tensor(x[:, bass.ds(half * HT, HT), :], x[:, bass.ds(half * HT, HT), :],
                                   bpb[:, :].unsqueeze(1).broadcast_to([P, HT, D]), ALU.add).then_inc(bias_added, 1)
            for half in range(HALVES):
                low_parts(half, 1)
            pool.iota(iota_b[:, :], [[1, BLOCKS]], base=0, channel_multiplier=0,
                      allow_small_or_imprecise_dtypes=True).then_inc(pool_step, 1)
            pool.wait_ge(xs_cleared, 16)
            pool.wait_ge(slots_ready, 1)
            for t in range(TILES):
                for k in range(TOPK):
                    pool.indirect_dma_start(xs, bass.IndirectOffsetOnAxis(ap=slot[:, t, k:k + 1], axis=0),
                                            xn4[:, t, :], None).then_inc(scattered, 16)
            for p in range(2):
                pool.wait_ge(y_stored[p], BLOCKS // 2 * 16)
            for n in range(TILES * TOPK):
                t, k = divmod(n, TOPK)
                if n >= YG:
                    pool.wait_ge(y_added, n - YG + 1)
                pool.indirect_dma_start(yg[:, n % YG, :], None, ys,
                                        bass.IndirectOffsetOnAxis(ap=slot[:, t, k:k + 1], axis=0)
                                        ).then_inc(gathered[n % YG], 16)

        @block.scalar
        def _(act):
            def deviation(half, n, k):
                act.wait_ge(var_ready[n], half * NORMS[n] + k + 1)
                act.activation(sd[:, 0:HT], var[:, 0:HT], ACT.Sqrt).then_inc(sd_ready[n], 1)

            def split(half, n):
                count = len(SPLITS[n])

                def middle(j):
                    rows = GROUPS * HD if n == 1 and SPLITS[n][j][1] == "K0" else P
                    job = JOB0[n] + LAYER_JOBS[n].index(SPLITS[n][j])
                    act.wait_ge(job_done[n], half * JOBS[n] + job + 1)
                    act.activation(parts[0:rows, j % RING[n], 1, :], rest[0:rows, j % RING[n], :],
                                   ACT.Copy).then_inc(mid_ready[n], 1)

                for j, (c, kind) in enumerate(SPLITS[n]):
                    slot = j % RING[n]
                    uses = len([i for i in range(count) if i % RING[n] == slot])
                    before = len([i for i in range(j) if i % RING[n] == slot])
                    job = LAYER_JOBS[n].index((c, kind))
                    if j >= RING[n]:
                        act.wait_ge(saved[n][slot], (half * uses + before) * 16)
                    act.wait_ge(job_ready[n], half * JOBS[n] + JOB0[n] + job + 1)
                    src = bank[(JOB0[n] + job) % JOB_BANKS]
                    if n == 0:
                        ins = act.activation(parts[:, slot, 0, :], src[:, :], ACT.Copy)
                    elif kind == "K0":
                        ins = act.activation(parts[0:GROUPS * HD, slot, 0, :], src[0:GROUPS * HD, :],
                                             ACT.Identity, bias=bk[:, :])
                    else:
                        m = int(kind[1])
                        ins = act.activation(parts[:, slot, 0, :], src[:, :], ACT.Identity, bias=bq[:, m:m + 1])
                    ins.then_inc(hi_ready[n], 1)
                    if j >= 1:
                        middle(j - 1)
                middle(count - 1)

            def copy_maxima(half, n, b):
                act.wait_ge(negT_ready[n], half * HS + b + 1)
                act.activation(negT[:, :], misc[0:2 * HEADS, 0:SEQ // 2].bitcast(BF16), ACT.Copy
                               ).then_inc(negT_copied[n], 1)

            def attention(half, n):
                width = 2 * SEQ if n == 0 else SEQ + P
                copy_maxima(half, n, 0)
                for b in range(HS):
                    for s in range(HEADS):
                        i = b * HEADS + s
                        act.wait_ge(st_ready[n], half * HS * HEADS + i + 1)
                        if i >= P_RING:
                            act.wait_ge(pv_ready[n], half * HS * HEADS + i - P_RING + 1)
                        act.activation(pt[:, i % P_RING, 0:width], st_bank[i % 3][:, 0:width], ACT.Exp,
                                       scale=HD ** -0.5).then_inc(exp_ready[n], 1)
                        if s == 11 and b + 1 < HS:
                            copy_maxima(half, n, b + 1)

            act.wait_ge(weights_loaded, 16 * len(WEIGHTS))
            for half in range(HALVES):
                deviation(half, 0, 0)
                split(half, 0)
                attention(half, 0)
            for half in range(HALVES):
                deviation(half, 1, 0)
                for t in range(HT):
                    act.wait_ge(xn_ready[1], half * 2 * HT + t + 1)
                    act.activation(pt[:, 0, 0:D], xn[:, t, :], ACT.Square,
                                   accum_out=xx[:, t:t + 1]).then_inc(squares_ready, 1)
                    act.wait_ge(squares_ready, half * HT + t + 1)
                act.wait_ge(logit_ready, half + 1)
                act.activation(sc[1][:, :, :], sc[0][:, :, :], ACT.Exp, scale=-1.0).then_inc(gate_exp_ready, 1)
                deviation(half, 1, 1)
                split(half, 1)
                attention(half, 1)
            act.wait_ge(var4_ready, 1)
            act.activation(sd[:, :], var[:, :], ACT.Sqrt).then_inc(sd4_ready, 1)
            act.wait_ge(route_ready, 1)
            act.activation(sbi, sp1, ACT.Exp).then_inc(route_act, 1)
            act.wait_ge(route_ready, 2)
            act.activation(sp1, sbi, ACT.Ln).then_inc(route_act, 1)
            act.wait_ge(route_ready, 3)
            act.activation(sco, sbi, ACT.Sqrt).then_inc(route_act, 1)
            for c in range(TOKENS // CHUNK):
                act.wait_ge(sgu_clipped, c + 1)
                act.activation(se, sg, ACT.Exp, scale=-1.0).then_inc(sexp_ready, 1)

            def copy_xbT(b, p):
                act.wait_ge(xb_turned, b + 1)
                act.activation(xbT[:, p, :, :].rearrange("p k t -> p (k t)"), bank[p][:, 0:D], ACT.Copy
                               ).then_inc(xbT_copied, 1)

            def gate_exp(b, p):
                act.wait_ge(gu_clipped, b + 1)
                act.activation(ge[:, p, :], gu[:, p, 0, :], ACT.Exp, scale=-1.0).then_inc(ge_ready, 1)

            def store_y(b, p, again):
                act.wait_ge(y_ready, b + 1)
                if again:
                    act.wait_ge(y_stored[p], pair_of(b, p) * 16)
                act.activation(yb[:, p, :], bank[6 + p][:, 0:D], ACT.Copy).then_inc(yb_copied, 1)
                act.wait_ge(yb_copied, b + 1)
                act.dma_start(ys[bass.ds(b * P, P), :], yb[:, p, :]).then_inc(y_stored[p], 16)

            def act_step(s, p):
                copy_xbT(s, p)
                gate_exp(s - 1, 1 - p)
                store_y(s - 3, 1 - p, True)

            copy_xbT(0, 0)
            copy_xbT(1, 1)
            gate_exp(0, 0)
            copy_xbT(2, 0)
            gate_exp(1, 1)
            copy_xbT(3, 1)
            gate_exp(2, 0)
            store_y(0, 0, False)
            copy_xbT(4, 0)
            gate_exp(3, 1)
            store_y(1, 1, False)
            act_step(5, 1)
            with act.Fori(3, BLOCKS // 2) as i:
                act_step(2 * i, 0)
                act_step(2 * i + 1, 1)
            gate_exp(BLOCKS - 1, 1)
            for b in range(BLOCKS - 3, BLOCKS):
                store_y(b, b % 2, True)

        @block.tensor
        def _(pe):
            pe.wait_ge(constants_made, CONSTANTS)
            pe.wait_ge(products_made, 1)
            for k in range(KD):
                mm_ = pe.matmul(bank[0][:, 0:FW], ones[:, :], prod[:, k, :], start=(k == 0), stop=(k == KD - 1))
            mm_.then_inc(sums_made, 1)

            def transposes(half, n, job, norm, c, k):
                pe.wait_ge(xn_ready[n], half * NORMS[n] * HT + norm * HT + (c + 1) * CT)
                for t in range(CT):
                    ins = pe.transpose(bank[job % JOB_BANKS][:, t * P:(t + 1) * P],
                                       xn[:, c * CT + t, k * P:(k + 1) * P], ident[:, :])
                ins.then_inc(job_ready[n], 1)

            def bank_free(half, n, job, first):
                if job - first >= JOB_BANKS:
                    pe.wait_ge(job_done[n], half * JOBS[n] + job - JOB_BANKS + 1)

            def project(half, n):
                w = (w0, w1)[n]
                kv = HEADS if n == 0 else GROUPS
                for i, (c, kind) in enumerate(LAYER_JOBS[n]):
                    job = JOB0[n] + i
                    b = bank[job % JOB_BANKS]
                    bank_free(half, n, job, JOB0[n])
                    at = slice(c * CHUNK, (c + 1) * CHUNK)
                    if kind[0] == "T":
                        transposes(half, n, job, n, c, int(kind[1]))
                        continue
                    if kind == "Q0":
                        pe.wait_ge(job_done[n], half * JOBS[n] + job)
                    if kind[0] in "QK":
                        col = (D if kind[0] == "K" else 0) + int(kind[1]) * P
                        rows = GROUPS * HD if n == 1 and kind == "K0" else P
                        for k in range(KD):
                            ins = pe.matmul(b[0:rows, :], w[:, k, col:col + rows], xnT[:, k, at],
                                            start=(k == 0), stop=(k == KD - 1))
                    else:
                        width = kv * HD
                        per = 512 // width if n == 0 else CT
                        for t in range(per):
                            tok = c * CHUNK + (int(kind[1]) * per + t) * P
                            for k in range(KD):
                                ins = pe.matmul(b[:, t * width:(t + 1) * width], xnT[:, k, tok:tok + P],
                                                w[:, k, D + width:D + 2 * width],
                                                start=(k == 0), stop=(k == KD - 1))
                    ins.then_inc(job_ready[n], 1)

            def unit(half, n, b, u):
                qt, h0, nh, nk = UNITS[n][u]
                i = b * len(UNITS[n]) + u
                if i >= 2:
                    pe.wait_ge(unit_done[n], half * HS * len(UNITS[n]) + i - 1)
                dst = unit_bank[i % 2]
                for a in range(nh):
                    ins = pe.matmul(dst[:, a * nk:(a + 1) * nk],
                                    qs[0:STACK, h0 + a, b * SEQ + qt * P:b * SEQ + (qt + 1) * P],
                                    ks[n][0:STACK, heads_of_kv(n, h0 + a), b * SEQ:b * SEQ + nk],
                                    start=True, stop=(n == 0))
                    if n == 1:
                        ins = pe.matmul(dst[:, a * nk + nk - P:(a + 1) * nk], identb[:, :], mask_s[:, :],
                                        start=False, stop=True)
                ins.then_inc(unit_ready[n], 1)

            def turn_maxima(half, n, b):
                pe.wait_ge(neg_ready[n], half * HS + b + 1)
                for qt in range(QT):
                    ins = pe.transpose(misc[0:2 * HEADS, qt * P // 2:(qt + 1) * P // 2].bitcast(BF16),
                                       neg[:, qt, :, :].rearrange("p a h -> p (a h)"), identb[:, :])
                ins.then_inc(negT_ready[n], 1)

            def scores(half, n, b, s):
                i = b * HEADS + s
                if i >= 3:
                    pe.wait_ge(exp_ready[n], half * HS * HEADS + i - 2)
                dst = st_bank[i % 3]
                kh = heads_of_kv(n, s)
                for kt in range(QT):
                    keys = ks[n][0:ROWS, kh, b * SEQ + kt * P:b * SEQ + (kt + 1) * P]
                    q0 = 0 if n == 0 or kt == 0 else P
                    at = kt * SEQ
                    ins = pe.matmul(dst[:, at:at + SEQ - q0], keys, qs[0:ROWS, s, b * SEQ + q0:(b + 1) * SEQ],
                                    start=True, stop=(n == 0))
                    if n == 1:
                        ins = pe.matmul(dst[:, at:at + P], identb[:, :], mask_t[:, :], start=False, stop=True)
                ins.then_inc(st_ready[n], 1)

            def values(half, n, i):
                b, h = divmod(i, HEADS)
                pe.wait_ge(exp_ready[n], half * HS * HEADS + i + 1)
                if h == 0:
                    pe.wait_ge(att_ready[n], half * HS + b) if b else None
                p = pt[:, i % P_RING, :]
                kh = heads_of_kv(n, h)
                for qt in range(QT):
                    kts = range(QT) if n == 0 else range(qt + 1)
                    for kt in kts:
                        col = kt * SEQ + qt * P if n == 0 or kt == 0 else SEQ
                        ins = pe.matmul(pv_bank[qt][:, h * VW:(h + 1) * VW], p[:, col:col + P],
                                        v[n][:, b * QT + kt, kh, :], start=(kt == 0), stop=(kt == kts[-1]))
                ins.then_inc(pv_ready[n], 1)

            def attention(half, n):
                units = len(UNITS[n])
                pe.wait_ge(job_done[n], (half + 1) * JOBS[n])
                pe.wait_ge(stacked[n][0], (half + 1) * 12 * 16)
                for u in range(units):
                    unit(half, n, 0, u)
                turn_maxima(half, n, 0)
                for b in range(HS):
                    pe.wait_ge(neg_stacked[n], (half * HS + b + 1) * 32)
                    if b == 1:
                        pe.wait_ge(stacked[n][1], (half + 1) * 12 * 16)
                    for s in range(HEADS):
                        scores(half, n, b, s)
                        if b * HEADS + s >= LAG:
                            values(half, n, b * HEADS + s - LAG)
                        if b + 1 < HS:
                            for u in range(2 * s, min(2 * s + 2, units)):
                                unit(half, n, b + 1, u)
                        if s == 11 and b + 1 < HS:
                            turn_maxima(half, n, b + 1)
                for i in range(HS * HEADS - LAG, HS * HEADS):
                    values(half, n, i)

            def out_project(half):
                pe.wait_ge(rows_moved, half + 1)
                job = 0
                for c in range(CHUNKS):
                    for k in range(KD):
                        for t in range(CT):
                            ins = pe.transpose(bank[job][:, t * P:(t + 1) * P],
                                               xn[:, c * CT + t, k * P:(k + 1) * P], ident[:, :])
                        ins.then_inc(job_ready[1], 1)
                        job += 1
                pe.wait_ge(job_done[1], half * JOBS[1] + job)
                for i in range(HT // 2):
                    bank_free(half, 1, job, 0)
                    for t in range(2):
                        for k in range(KD):
                            ins = pe.matmul(bank[job % JOB_BANKS][:, t * D:(t + 1) * D],
                                            xnT[:, k, (2 * i + t) * P:(2 * i + t + 1) * P], wp[:, k, :],
                                            start=(k == 0), stop=(k == KD - 1))
                    ins.then_inc(job_ready[1], 1)
                    job += 1

            def select(half):
                job = JOB_F
                for c in range(CHUNKS):
                    for k in range(KD):
                        bank_free(half, 1, job, 0)
                        transposes(half, 1, job, 0, c, k)
                        job += 1
                pe.wait_ge(job_done[1], half * JOBS[1] + job)
                for i in range(HT // 2):
                    bank_free(half, 1, job, 0)
                    for t in range(2):
                        for k in range(KD):
                            ins = pe.matmul(bank[job % JOB_BANKS][:, t * FW:(t + 1) * FW],
                                            xnT[:, k, (2 * i + t) * P:(2 * i + t + 1) * P], wf[:, k, :],
                                            start=(k == 0), stop=(k == KD - 1))
                    ins.then_inc(job_ready[1], 1)
                    job += 1
                pe.wait_ge(selected, half + 1)
                for c in range(CHUNKS):
                    bank_free(half, 1, job, 0)
                    for t in range(CT):
                        ins = pe.transpose(bank[job % JOB_BANKS][0:MW, t * P:(t + 1) * P],
                                           mm[:, c * CT + t, :], ident[:, :])
                    ins.then_inc(job_ready[1], 1)
                    job += 1
                pe.wait_ge(job_done[1], half * JOBS[1] + job)
                for i in range(HT // 2):
                    bank_free(half, 1, job, 0)
                    for t in range(2):
                        ins = pe.matmul(bank[job % JOB_BANKS][:, t * D:(t + 1) * D],
                                        mT[:, (2 * i + t) * P:(2 * i + t + 1) * P], wd[:, :],
                                        start=True, stop=True)
                    ins.then_inc(job_ready[1], 1)
                    job += 1

            pe.wait_ge(sums_copied, 1)
            for half in range(HALVES):
                pe.wait_ge(att_ready[0], half * HS)
                project(half, 0)
                attention(half, 0)
            for half in range(HALVES):
                pe.wait_ge(att_ready[1], half * HS)
                out_project(half)
                select(half)
                project(half, 1)
                attention(half, 1)
            for n in range(TOKENS // CHUNK * KD):
                c, k = divmod(n, KD)
                pe.wait_ge(xn4_ready, (c + 1) * CT)
                if n >= 4:
                    pe.wait_ge(turn4_copied, n - 3)
                for t in range(CT):
                    ins = pe.transpose(bank[n % 4][:, t * P:(t + 1) * P],
                                       xn4[:, c * CT + t, k * P:(k + 1) * P], ident[:, :])
                ins.then_inc(turn4_ready, 1)
            pe.wait_ge(turn4_copied, TOKENS // CHUNK * KD)
            for t in range(TILES):
                for k in range(KD):
                    ins = pe.matmul(bank[6][:, t * EXPERTS:(t + 1) * EXPERTS], xnT4[:, k, t * P:(t + 1) * P],
                                    wr[:, k, :], start=(k == 0), stop=(k == KD - 1))
            ins.then_inc(logits_ready, 1)

            def ranks():
                pe.wait_ge(chosen_ready, 1)
                all_c = chosen[:, :, :].rearrange("p t e -> p (t e)")
                for t in range(1, TILES):
                    pe.matmul(bank[7][:, t * EXPERTS:te], onesb[:, :], all_c[:, 0:te - t * EXPERTS],
                              start=(t == 1), stop=False, skip_group_check=True)
                pe.matmul(bank[7][:, :], before[:, :], all_c, start=False, stop=True, skip_group_check=True)
                for t in range(TILES):
                    ins = pe.matmul(bank[5][:, 0:EXPERTS], onesb[:, :], chosen[:, t, :],
                                    start=(t == 0), stop=(t == TILES - 1))
                ins.then_inc(ranks_ready, 1)

            def shared_up(c):
                if c >= 1:
                    pe.wait_ge(sgu_clipped, c)
                for j in range(2):
                    for k in range(KD):
                        at0 = k * 2 * INNER + j * INNER
                        ins = pe.matmul(bank[j][:, :], wsh[:, at0:at0 + INNER],
                                        xnT4[:, k, c * CHUNK:(c + 1) * CHUNK], start=(k == 0), stop=(k == KD - 1))
                ins.then_inc(sgu_ready, 1)

            def shared_down(c):
                pe.wait_ge(shid_ready, c + 1)
                for j in range(2):
                    n = 2 * c + j
                    if n >= 2:
                        pe.wait_ge(sdown_added, n - 1)
                    for t in range(2):
                        at0 = (2 * j + t) * P
                        ins = pe.matmul(bank[2 + j][:, t * D:(t + 1) * D], sh[:, at0:at0 + P],
                                        wsh[:, 2 * KD * INNER:EW], start=True, stop=True)
                    ins.then_inc(sdown_ready, 1)

            ranks()
            for c in range(TOKENS // CHUNK):
                shared_up(c)
                shared_down(c)

            pe.wait_ge(experts_loaded, 16)
            pe.wait_ge(blocks_ready, 1)
            pe.wait_ge(sdown_added, TOKENS // CHUNK * 2)

            def turn_block(b, p, again):
                pe.wait_ge(xb_loaded[p], (pair_of(b, p) + 1) * 16)
                if again:
                    pe.wait_ge(xbT_copied, b - 1)
                for k in range(KD):
                    ins = pe.transpose(bank[p][:, k * P:(k + 1) * P], xb[:, p, k * P:(k + 1) * P], ident[:, :])
                ins.then_inc(xb_turned, 1)

            def expert_of(b):
                return pe.value_load(eb_i[0:1, bass.ds(b, 1)], min_val=0, max_val=EXPERTS - 1)

            def gate_up(b, p, again):
                e = expert_of(b)
                pe.wait_ge(xbT_copied, b + 1)
                if again:
                    pe.wait_ge(gu_clipped, b - 1)
                for k in range(KD):
                    ins = pe.matmul(bank[2 + p][:, 0:2 * INNER], xbT[:, p, k, :],
                                    arena[:, bass.ds(e * EW + k * 2 * INNER, 2 * INNER)],
                                    start=(k == 0), stop=(k == KD - 1))
                ins.then_inc(gu_ready, 1)

            def turn_hidden(b, p, again):
                pe.wait_ge(hid_ready, b + 1)
                if again:
                    pe.wait_ge(hidT_copied, b - 1)
                pe.transpose(bank[4 + p][:, 0:P], hid[:, p, :], ident[:, :]).then_inc(hid_turned, 1)

            def down(b, p, again):
                e = expert_of(b)
                pe.wait_ge(hidT_copied, b + 1)
                if again:
                    pe.wait_ge(yb_copied, b - 1)
                pe.matmul(bank[6 + p][:, 0:D], hidT[:, p, :], arena[:, bass.ds(e * EW + 2 * KD * INNER, D)],
                          start=True, stop=True).then_inc(y_ready, 1)

            def pe_step(s, p):
                turn_block(s, p, True)
                gate_up(s - 1, 1 - p, True)
                turn_hidden(s - 2, p, True)
                down(s - 3, 1 - p, True)

            for s in range(6):
                turn_block(s, s % 2, s >= 2)
                if s >= 1:
                    gate_up(s - 1, (s - 1) % 2, s >= 3)
                if s >= 2:
                    turn_hidden(s - 2, s % 2, s >= 4)
                if s >= 3:
                    down(s - 3, (s - 3) % 2, s >= 5)
            with pe.Fori(3, BLOCKS // 2) as i:
                pe_step(2 * i, 0)
                pe_step(2 * i + 1, 1)
            for s in range(BLOCKS, BLOCKS + 3):
                if s - 1 < BLOCKS:
                    gate_up(s - 1, (s - 1) % 2, True)
                if s - 2 < BLOCKS:
                    turn_hidden(s - 2, s % 2, True)
                down(s - 3, (s - 3) % 2, True)

        @block.vector
        def _(dve):
            for n in range(2):
                dve.memset(ks[n][STACK:ROWS, :, :], 1.0).then_inc(constants_made, 1)
            dve.wait_ge(weights_loaded, 16 * len(WEIGHTS))
            sel_w = wf[:, :, 0:NSEL * SELW].rearrange("p k (n s) -> p k n s", s=SELW)
            dif_w = wf[:, :, NSEL * SELW:NSEL * SELW + NSEL]
            upd_w = wf[:, :, NSEL * SELW + NSEL:FW].rearrange("p k (n s) -> p k n s", s=LORA)
            for k in range(KD):
                dve.tensor_tensor(prod[:, k, 0:NSEL * SELW].rearrange("p (n s) -> p n s", s=SELW), sel_w[:, k],
                                  dif_w[:, k].unsqueeze(2).broadcast_to([P, NSEL, SELW]), ALU.mult)
                dve.scalar_tensor_tensor(out=prod[:, k, NSEL * SELW:NSEL * SELW + NSEL], in0=dif_w[:, k],
                                         scalar=0.5, in1=dif_w[:, k], op0=ALU.mult, op1=ALU.mult)
                ins = dve.tensor_tensor(prod[:, k, NSEL * SELW + NSEL:FW].rearrange("p (n s) -> p n s", s=LORA),
                                        upd_w[:, k], wdb[:, k].unsqueeze(2).broadcast_to([P, NSEL, LORA]), ALU.mult)
            ins.then_inc(products_made, 1)
            dve.wait_ge(sums_made, 1)
            dve.tensor_copy(constb[:, :], bank[0][:, 0:FW]).then_inc(sums_copied, 1)
            dve.wait_ge(constants_made, CONSTANTS)
            dve.wait_ge(sums_copied, 1)

            steps = [0]

            def step(half, n, ins):
                steps[0] += 1
                ins.then_inc(dve_step[n], 1)
                dve.wait_ge(dve_step[n], half * DVE_STEPS[n] + steps[0])

            def norm(half, n, k):
                for t in range(HT):
                    ins = dve.bn_stats(st[:, t, :], x[:, half * HT + t, :])
                step(half, n, ins)
                for t in range(HT):
                    ins = dve.bn_aggr(mv[:, t, :], st[:, t, :])
                step(half, n, ins)
                dve.tensor_scalar(var[:, 0:HT], mv[:, 0:HT, 1], EPS, None, ALU.add).then_inc(var_ready[n], 1)
                dve.wait_ge(sd_ready[n], half * NORMS[n] + k + 1)
                step(half, n, dve.reciprocal(rstd[:, 0:HT], sd[:, 0:HT]))
                for t in range(HT):
                    dve.tensor_scalar(xn[:, t, :], x[:, half * HT + t, :], mv[:, t, 0:1], rstd[:, t:t + 1],
                                      ALU.subtract, ALU.mult).then_inc(xn_ready[n], 1)

            def turn_copy(half, n, job, c, k):
                dve.wait_ge(job_ready[n], half * JOBS[n] + job + 1)
                dve.tensor_copy(xnT[:, k, c * CHUNK:(c + 1) * CHUNK], bank[job % JOB_BANKS][:, :]
                                ).then_inc(job_done[n], 1)

            def project(half, n):
                kv = HEADS if n == 0 else GROUPS
                for i, (c, kind) in enumerate(LAYER_JOBS[n]):
                    job = JOB0[n] + i
                    b = bank[job % JOB_BANKS]
                    if kind[0] == "T":
                        turn_copy(half, n, job, c, int(kind[1]))
                    elif kind[0] in "QK":
                        j = SPLITS[n].index((c, kind))
                        slot = j % RING[n]
                        rows = GROUPS * HD if n == 1 and kind == "K0" else P
                        dve.wait_ge(hi_ready[n], half * len(SPLITS[n]) + j + 1)
                        if j >= RING[n]:
                            dve.wait_ge(low_ready[n], half * len(SPLITS[n]) + j - RING[n] + 1)
                        if n == 0:
                            ins = dve.tensor_tensor(rest[:, slot, :], b[:, :], parts[:, slot, 0, :], ALU.subtract)
                        else:
                            bias = bk[:, :] if kind == "K0" else bq[:, int(kind[1]):int(kind[1]) + 1]
                            ins = dve.scalar_tensor_tensor(out=rest[0:rows, slot, :], in0=b[0:rows, :], scalar=bias,
                                                           in1=parts[0:rows, slot, 0, :],
                                                           op0=ALU.add, op1=ALU.subtract)
                        ins.then_inc(job_done[n], 1)
                    else:
                        width = kv * HD
                        per = 512 // width if n == 0 else CT
                        dve.wait_ge(job_ready[n], half * JOBS[n] + job + 1)
                        tile = c * CT + int(kind[1]) * per
                        src = b[:, 0:per * width].rearrange("p (t h d) -> p t h d", t=per, d=HD)
                        for t in range(per):
                            if n == 0:
                                ins = dve.tensor_copy(v[0][:, tile + t, :, 0:HD], src[:, t])
                            else:
                                ins = dve.tensor_tensor(v[1][:, tile + t, :, 0:HD], src[:, t],
                                                        bvb[:, :].rearrange("p (h d) -> p h d", d=HD), ALU.add)
                        ins.then_inc(job_done[n], 1)

            def unit(half, n, b, u):
                qt, h0, nh, nk = UNITS[n][u]
                i = b * len(UNITS[n]) + u
                dve.wait_ge(unit_ready[n], half * HS * len(UNITS[n]) + i + 1)
                dve.tensor_reduce(mx[:, qt, h0:h0 + nh],
                                  unit_bank[i % 2][:, 0:nh * nk].rearrange("p (h k) -> p h k", h=nh),
                                  AX.X, ALU.max).then_inc(unit_done[n], 1)

            def minus_maxima(half, n, b):
                dve.wait_ge(unit_done[n], (half * HS + b + 1) * len(UNITS[n]))
                step(half, n, dve.tensor_scalar(neg[:, :, 0, :], mx[:, :, :], -1.0, None, ALU.mult))
                dve.scalar_tensor_tensor(out=neg[:, :, 1, :], in0=mx[:, :, :], scalar=-1.0, in1=neg[:, :, 0, :],
                                         op0=ALU.mult, op1=ALU.subtract).then_inc(neg_ready[n], 1)

            def divide(half, n, b):
                dve.wait_ge(pv_ready[n], (half * HS + b + 1) * HEADS)
                for qt in range(QT):
                    pv = pv_bank[qt][:, 0:HEADS * VW].rearrange("p (h d) -> p h d", d=VW)
                    ins = dve.reciprocal(rec[:, qt, :], pv[:, :, HD])
                step(half, n, ins)
                for qt in range(QT):
                    if n == 0:
                        for e in range(2):
                            heads = slice(e * SEQS, (e + 1) * SEQS)
                            pv = pv_bank[qt][:, 0:HEADS * VW].rearrange("p (h d) -> p h d", d=VW)[:, heads, 0:HD]
                            ins = dve.tensor_tensor(ctx0[:, :, qt, bass.ds(half * 2 * HS + 2 * b + e, 1), :]
                                                    .rearrange("p j o d -> p j (o d)"), pv,
                                                    rec[:, qt, heads].unsqueeze(2).broadcast_to([P, SEQS, HD]),
                                                    ALU.mult)
                    else:
                        pv = pv_bank[qt][:, 0:HEADS * VW].rearrange("p (h d) -> p h d", d=VW)
                        ins = dve.tensor_tensor(att[:, qt, :].rearrange("p (h d) -> p h d", d=HD), pv[:, :, 0:HD],
                                                rec[:, qt, :].unsqueeze(2).broadcast_to([P, HEADS, HD]), ALU.mult)
                ins.then_inc(att_ready[n], 1)
                if n == 1:
                    dve.wait_ge(att_ready[1], half * HS + b + 1)
                    xb = x[:, bass.ds(half * HT + b * QT, QT), :]
                    ins = dve.tensor_tensor(xb, xb, att[:, :, :], ALU.add)
                    if b == HS - 1:
                        step(half, n, ins)

            def attention(half, n):
                units = len(UNITS[n])
                for u in range(units):
                    unit(half, n, 0, u)
                minus_maxima(half, n, 0)
                for b in range(HS):
                    for s in range(HEADS):
                        if b > 0 and s == LAG:
                            divide(half, n, b - 1)
                        if b + 1 < HS:
                            for u in range(2 * s, min(2 * s + 2, units)):
                                unit(half, n, b + 1, u)
                            if 2 * s + 2 == units:
                                minus_maxima(half, n, b + 1)
                divide(half, n, HS - 1)

            def add_pairs(half, job):
                for i in range(HT // 2):
                    dve.wait_ge(job_ready[1], half * JOBS[1] + job + 1)
                    xb = x[:, bass.ds(half * HT + 2 * i, 2), :]
                    dve.tensor_tensor(xb, xb, bank[job % JOB_BANKS][:, :].rearrange("p (t d) -> p t d", t=2),
                                      ALU.add).then_inc(job_done[1], 1)
                    job += 1
                dve.wait_ge(job_done[1], half * JOBS[1] + job)

            def out_project(half):
                dve.wait_ge(bias_added, HALVES)
                dve.wait_ge(att_ready[0], SEQS)
                dve.tensor_copy(xn[:, :, :], ctx0[:, bass.ds(half * HS, HS), :, :, :]
                                .rearrange("p s q h d -> p (s q) (h d)")).then_inc(rows_moved, 1)
                for c in range(CHUNKS):
                    for k in range(KD):
                        turn_copy(half, 1, c * KD + k, c, k)
                add_pairs(half, CHUNKS * KD)

            def select(half):
                job = JOB_F
                for c in range(CHUNKS):
                    for k in range(KD):
                        turn_copy(half, 1, job, c, k)
                        job += 1
                for i in range(HT // 2):
                    dve.wait_ge(job_ready[1], half * JOBS[1] + job + 1)
                    dve.tensor_tensor(g[:, 2 * i:2 * i + 2, :],
                                      bank[job % JOB_BANKS][:, 0:2 * FW].rearrange("p (t f) -> p t f", t=2),
                                      constb[:, :].unsqueeze(1).broadcast_to([P, 2, FW]), ALU.subtract
                                      ).then_inc(job_done[1], 1)
                    job += 1
                dve.wait_ge(job_done[1], half * JOBS[1] + job)
                a = NSEL * SELW
                wide = [P, HT, NSEL]

                def row(t):
                    return t[:, :].unsqueeze(2).broadcast_to(wide)

                def col(t):
                    return t[:, :].unsqueeze(1).broadcast_to(wide)

                dve.wait_ge(squares_ready, (half + 1) * HT)
                dve.scalar_tensor_tensor(out=sc[2][:, :, :], in0=g[:, :, a:a + NSEL], scalar=-2.0, in1=row(xx),
                                         op0=ALU.mult, op1=ALU.add)
                step(half, 1, dve.tensor_tensor(sq[:, :, :], g[:, :, 0:a], g[:, :, 0:a], ALU.mult))
                dve.reciprocal(sc[3][:, :, :], sc[2][:, :, :])
                step(half, 1, dve.tensor_reduce(sc[0][:, :, :], sq[:, :, :].rearrange("p t (n s) -> p t n s", s=SELW),
                                             AX.X, ALU.add))
                step(half, 1, dve.tensor_tensor(sc[1][:, :, :], sc[0][:, :, :], sc[3][:, :, :], ALU.mult))
                step(half, 1, dve.tensor_tensor(sc[2][:, :, :], sc[1][:, :, :], col(cenb), ALU.subtract))
                step(half, 1, dve.tensor_tensor(sc[3][:, :, :], sc[2][:, :, :], col(slob), ALU.mult))
                dve.tensor_scalar(sc[0][:, :, :], sc[3][:, :, :], -80.0, None, ALU.max).then_inc(logit_ready, 1)
                dve.wait_ge(gate_exp_ready, half + 1)
                step(half, 1, dve.tensor_scalar(sc[2][:, :, :], sc[1][:, :, :], 1.0, None, ALU.add))
                step(half, 1, dve.reciprocal(sc[3][:, :, :], sc[2][:, :, :]))
                step(half, 1, dve.tensor_reduce(top[:, :], sc[3][:, :, :], AX.X, ALU.max))
                dve.tensor_scalar(keep[:, :], top[:, :], -1.0, 1.0, ALU.mult, ALU.add)
                step(half, 1, dve.tensor_tensor(sc[0][:, :, :], sc[3][:, :, :], row(top), ALU.is_equal))
                step(half, 1, dve.scalar_tensor_tensor(out=sc[1][:, :, :], in0=sc[0][:, :, :], scalar=-float(NSEL),
                                                    in1=col(iota8), op0=ALU.mult, op1=ALU.add))
                step(half, 1, dve.tensor_reduce(least[:, :], sc[1][:, :, :], AX.X, ALU.min))
                step(half, 1, dve.tensor_tensor(sc[2][:, :, :], sc[1][:, :, :], row(least), ALU.is_equal))
                step(half, 1, dve.tensor_tensor(mm[:, :, NSEL * LORA:MW], sc[2][:, :, :], row(top), ALU.mult))
                for t in range(HT):
                    dve.tensor_tensor(mm[:, t, 0:NSEL * LORA].rearrange("p (n h) -> p n h", h=LORA),
                                      g[:, t, a + NSEL:FW].rearrange("p (n h) -> p n h", h=LORA),
                                      mm[:, t, NSEL * LORA:MW].unsqueeze(2).broadcast_to([P, NSEL, LORA]), ALU.mult)
                    ins = dve.scalar_tensor_tensor(out=x[:, half * HT + t, :], in0=xn[:, t, :],
                                                   scalar=keep[:, t:t + 1], in1=x[:, half * HT + t, :],
                                                   op0=ALU.mult, op1=ALU.add)
                ins.then_inc(selected, 1)
                for c in range(CHUNKS):
                    dve.wait_ge(job_ready[1], half * JOBS[1] + job + 1)
                    dve.tensor_copy(mT[:, c * CHUNK:(c + 1) * CHUNK], bank[job % JOB_BANKS][0:MW, :]
                                    ).then_inc(job_done[1], 1)
                    job += 1
                dve.wait_ge(selected, half + 1)
                add_pairs(half, job)

            for half in range(HALVES):
                steps[0] = 0
                dve.wait_ge(x_loaded, (half + 1) * 16)
                norm(half, 0, 0)
                project(half, 0)
                attention(half, 0)
                assert steps[0] == DVE_STEPS[0], steps[0]
            for half in range(HALVES):
                steps[0] = 0
                out_project(half)
                norm(half, 1, 0)
                select(half)
                norm(half, 1, 1)
                project(half, 1)
                attention(half, 1)
                assert steps[0] == DVE_STEPS[1], steps[0]
            moe_steps = [0]

            def then(ins):
                moe_steps[0] += 1
                ins.then_inc(moe_step, 1)
                dve.wait_ge(moe_step, moe_steps[0])

            for t in range(TILES):
                ins = dve.bn_stats(st[:, t, :], x[:, t, :])
            then(ins)
            for t in range(TILES):
                ins = dve.bn_aggr(mv[:, t, :], st[:, t, :])
            then(ins)
            dve.tensor_scalar(var[:, :], mv[:, :, 1], EPS, None, ALU.add).then_inc(var4_ready, 1)
            dve.wait_ge(sd4_ready, 1)
            then(dve.reciprocal(rstd[:, :], sd[:, :]))
            for t in range(TILES):
                dve.tensor_scalar(xn4[:, t, :], x[:, t, :], mv[:, t, 0:1], rstd[:, t:t + 1],
                                  ALU.subtract, ALU.mult).then_inc(xn4_ready, 1)
            for n in range(TOKENS // CHUNK * KD):
                c, k = divmod(n, KD)
                dve.wait_ge(turn4_ready, n + 1)
                dve.tensor_copy(xnT4[:, k, c * CHUNK:(c + 1) * CHUNK], bank[n % 4][:, :]).then_inc(turn4_copied, 1)

            dve.wait_ge(logits_ready, 1)
            then(dve.tensor_copy(lg, bank[6][:, :].rearrange("p (t e) -> p t e", t=TILES)))
            dve.scalar_tensor_tensor(out=sp1, in0=lg, scalar=-1.0, in1=lg, op0=ALU.mult, op1=ALU.min
                                     ).then_inc(route_ready, 1)
            dve.wait_ge(route_act, 1)
            dve.tensor_scalar(sbi, sbi, 1.0, None, ALU.add).then_inc(route_ready, 1)
            dve.wait_ge(route_act, 2)
            dve.scalar_tensor_tensor(out=sbi, in0=lg, scalar=0.0, in1=sp1, op0=ALU.max, op1=ALU.add
                                     ).then_inc(route_ready, 1)
            dve.wait_ge(route_act, 3)
            by_tile = [P, TILES, EXPERTS]
            by_pick = [P, TILES, TOPK, EXPERTS]
            then(dve.tensor_tensor(sbi, sco, ebb[:, :].unsqueeze(1).broadcast_to(by_tile), ALU.add))
            for t in range(TILES):
                ins = dve.max(m8[:, t, :], sbi[:, t, :])
            then(ins)
            for t in range(TILES):
                ins = dve.max_index(i8[:, t, :], m8[:, t, :], sbi[:, t, :])
            then(ins)
            then(dve.tensor_copy(pk[0][:, :, :], i8[:, :, 0:TOPK]))
            then(dve.tensor_tensor(pick[:, :, :, :],
                                   iota32[:, :].unsqueeze(1).unsqueeze(1).broadcast_to(by_pick),
                                   pk[0][:, :, :].unsqueeze(3).broadcast_to(by_pick), ALU.is_equal))
            with nc.allow_low_precision("sums of four zeros and ones"):
                dve.tensor_reduce(chosen[:, :, :], pick[:, :, :, :].rearrange("p t k e -> p t e k"),
                                  AX.X, ALU.add).then_inc(chosen_ready, 1)
            then(dve.tensor_tensor(work, pick[:, :, :, :], sco.unsqueeze(2).broadcast_to(by_pick), ALU.mult))
            then(dve.tensor_reduce(pk[0][:, :, :], work, AX.X, ALU.add))
            then(dve.tensor_reduce(ps[0][:, :], pk[0][:, :, :], AX.X, ALU.add))
            then(dve.tensor_scalar(ps[1][:, :], ps[0][:, :], 1e-20, None, ALU.add))
            then(dve.reciprocal(ps[0][:, :], ps[1][:, :]))
            then(dve.tensor_tensor(pk[1][:, :, :], pk[0][:, :, :],
                                   ps[0][:, :].unsqueeze(2).broadcast_to([P, TILES, TOPK]), ALU.mult))
            dve.wait_ge(ranks_ready, 1)
            then(dve.tensor_scalar(cnti[0][:, :], bank[5][:, 0:EXPERTS], float(P - 1), None, ALU.add))
            then(dve.tensor_scalar(cnti[1][:, :], cnti[0][:, :], P.bit_length() - 1, None, ALU.logical_shift_right))
            then(dve.tensor_copy(cnt[0][:, :], cnti[1][:, :]))
            ee = [P, EXPERTS, EXPERTS]
            pair = exps[:, 0:EXPERTS * EXPERTS].rearrange("p (e f) -> p e f", e=EXPERTS)
            then(dve.tensor_tensor(pair, iota32[:, :].unsqueeze(2).broadcast_to(ee),
                                   iota32[:, :].unsqueeze(1).broadcast_to(ee), ALU.is_gt))
            then(dve.tensor_tensor(pair, pair, cnt[0][:, :].unsqueeze(1).broadcast_to(ee), ALU.mult))
            then(dve.tensor_reduce(cnt[1][:, :], pair, AX.X, ALU.add))
            then(dve.tensor_tensor(cnt[2][:, :], cnt[0][:, :], cnt[1][:, :], ALU.add))
            then(dve.tensor_scalar(cnt[3][:, :], cnt[1][:, :], float(P), None, ALU.mult))
            then(dve.tensor_tensor(slots_e, bank[7][:, :].rearrange("p (t e) -> p t e", t=TILES),
                                   cnt[3][:, :].unsqueeze(1).broadcast_to(by_tile), ALU.add))
            then(dve.tensor_tensor(work, pick[:, :, :, :], slots_e.unsqueeze(2).broadcast_to(by_pick), ALU.mult))
            then(dve.tensor_reduce(pk[0][:, :, :], work, AX.X, ALU.add))
            dve.tensor_copy(slot[:, :, :], pk[0][:, :, :]).then_inc(slots_ready, 1)
            dve.wait_ge(pool_step, 6)
            half_b = BLOCKS // 2
            be = [1, half_b, EXPERTS]
            for i in range(2):
                rows = slice(i * half_b, (i + 1) * half_b)
                over = exps[0:1, 0:half_b * EXPERTS].rearrange("p (b e) -> p b e", b=half_b)
                then(dve.tensor_tensor(over, cnt[2][0:1, :].unsqueeze(1).broadcast_to(be),
                                       iota_b[:, rows].unsqueeze(2).broadcast_to(be), ALU.is_le))
                then(dve.tensor_reduce(eb_f[:, rows], over, AX.X, ALU.add))
            dve.tensor_scalar(eb_i[:, :], eb_f[:, :], float(EXPERTS - 1), None, ALU.min).then_inc(blocks_ready, 1)

            for c in range(TOKENS // CHUNK):
                dve.wait_ge(sgu_ready, c + 1)
                if c:
                    dve.wait_ge(sexp_ready, c)
                dve.tensor_scalar(sg, bank[0][:, :], CLAMP, -CLAMP, ALU.min, ALU.max)
                dve.tensor_scalar(su, bank[1][:, :], CLAMP, -CLAMP, ALU.min, ALU.max).then_inc(sgu_clipped, 1)
                dve.wait_ge(sgu_clipped, c + 1)
                then(dve.tensor_tensor(su, sg, su, ALU.mult))
                dve.wait_ge(sexp_ready, c + 1)
                then(dve.tensor_scalar(se, se, 1.0, None, ALU.add))
                then(dve.reciprocal(se, se))
                dve.tensor_tensor(sh, su, se, ALU.mult).then_inc(shid_ready, 1)
                for j in range(2):
                    dve.wait_ge(sdown_ready, 2 * c + j + 1)
                    xt = x[:, c * CT + 2 * j:c * CT + 2 * j + 2, :]
                    dve.tensor_tensor(xt, xt, bank[2 + j][:, :].rearrange("p (t d) -> p t d", t=2), ALU.add
                                      ).then_inc(sdown_added, 1)

            def clip(b, p):
                dve.wait_ge(gu_ready, b + 1)
                dve.tensor_scalar(gu[:, p, :, :].rearrange("p g i -> p (g i)"), bank[2 + p][:, 0:2 * INNER],
                                  CLAMP, -CLAMP, ALU.min, ALU.max).then_inc(gu_clipped, 1)

            def hidden(b, p):
                dve.wait_ge(ge_ready, b + 1)
                dve.tensor_tensor(gu[:, p, 1, :], gu[:, p, 0, :], gu[:, p, 1, :], ALU.mult)
                dve.tensor_scalar(ge[:, p, :], ge[:, p, :], 1.0, None, ALU.add).then_inc(hid_step, 1)
                dve.wait_ge(hid_step, 2 * b + 1)
                dve.reciprocal(ge[:, p, :], ge[:, p, :]).then_inc(hid_step, 1)
                dve.wait_ge(hid_step, 2 * b + 2)
                dve.tensor_tensor(hid[:, p, :], gu[:, p, 1, :], ge[:, p, :], ALU.mult).then_inc(hid_ready, 1)

            def copy_hidden(b, p):
                dve.wait_ge(hid_turned, b + 1)
                dve.tensor_copy(hidT[:, p, :], bank[4 + p][:, 0:P]).then_inc(hidT_copied, 1)

            def dve_step_moe(s, p):
                clip(s - 1, 1 - p)
                hidden(s - 1, 1 - p)
                copy_hidden(s - 2, p)

            clip(0, 0)
            hidden(0, 0)
            for s in range(2, 6):
                dve_step_moe(s, s % 2)
            with dve.Fori(3, BLOCKS // 2) as i:
                dve_step_moe(2 * i, 0)
                dve_step_moe(2 * i + 1, 1)
            dve_step_moe(BLOCKS, 0)
            copy_hidden(BLOCKS - 1, 1)

            for n in range(TILES * TOPK):
                t, k = divmod(n, TOPK)
                dve.wait_ge(gathered[n % YG], (n // YG + 1) * 16)
                if k:
                    dve.wait_ge(y_added, n)
                dve.scalar_tensor_tensor(out=x[:, t, :], in0=yg[:, n % YG, :], scalar=pk[1][:, t, k:k + 1],
                                         in1=x[:, t, :], op0=ALU.mult, op1=ALU.add).then_inc(y_added, 1)


_SHAPES = "inputs as laid out below"


def _layout(i):
    a = {n: np.asarray(v) for n, v in i.items()}
    qkv = a["L0_attn_Wqkv"].reshape(HEADS, 3, HD, D).transpose(3, 1, 0, 2).reshape(D, 3 * D)

    def flat(w):
        return w.transpose(1, 0, 2).reshape(w.shape[1], -1)

    ffn = np.concatenate([flat(a["L0_ffn_select_weight"]), a["L0_ffn_select_mean_diff"].T,
                          flat(a["L0_ffn_lora_update"])], axis=1)
    down = np.concatenate([a["L0_ffn_lora_degen"].transpose(0, 2, 1).reshape(NSEL * LORA, D), a["L0_ffn_bias_w"]])
    qkv1 = np.concatenate([flat(a["L1_attn_Wq"]), flat(a["L1_attn_Wk"]), flat(a["L1_attn_Wv"])], axis=1)

    def halves(w):
        return w.reshape(w.shape[0], INNER, KD, P).transpose(0, 3, 2, 1)

    gate = np.concatenate([a["L1_ffn_gate_w"], a["L1_ffn_shared_gate_w"][None]])
    up = np.concatenate([a["L1_ffn_up_w"], a["L1_ffn_shared_up_w"][None]])
    dn = np.concatenate([a["L1_ffn_down_w"], a["L1_ffn_shared_down_w"][None]])
    gu = np.concatenate([halves(gate), halves(up)], axis=3).reshape(EXPERTS + 1, P, 2 * KD * INNER)
    experts = np.concatenate([gu, dn.transpose(0, 2, 1)], axis=2).transpose(1, 0, 2)
    return [a["L0_attn_query"].reshape(TOKENS, D), qkv, a["L0_attn_Wproj"].T, a["L0_attn_bproj"].reshape(1, D),
            ffn, a["L0_ffn_debias_w"].T, down, a["L0_ffn_imp_center"].reshape(1, NSEL),
            a["L0_ffn_imp_slope"].reshape(1, NSEL), qkv1, a["L1_attn_bq"].reshape(KD, P).T,
            a["L1_attn_bk"].reshape(GROUPS * HD, 1), a["L1_attn_bv"].reshape(1, GROUPS * HD),
            a["L1_ffn_router_w"].T, a["L1_ffn_expert_bias"].reshape(1, EXPERTS), experts]


def kernel(**inputs):
    import concourse.bacc as bacc
    from concourse.bass_utils import run_bass_kernel_spmd

    nc = bacc.Bacc("TRN2", target_bir_lowering=False, num_devices=1)
    arrays, args = {}, []
    for n, a in enumerate(_layout(inputs)):
        a = np.ascontiguousarray(a)
        arrays[f"in_{n}"] = a
        args.append(nc.dram_tensor(f"in_{n}", a.shape, mybir.dt.from_np(a.dtype), kind="ExternalInput").ap())
    args.append(nc.dram_tensor("out", (TOKENS, D), F32, kind="ExternalOutput").ap())
    nc.disable_value_cache = True
    two_block_kernel(nc, *args)
    r = run_bass_kernel_spmd(nc, [arrays], core_ids=[0])
    return r.results[0]["out"].reshape(SEQS, SEQ, D)
```

```python
from contextlib import ExitStack

import numpy as np
import concourse.bass as bass
from concourse import mybir

ALU = mybir.AluOpType
ACT = mybir.ActivationFunctionType
AX = mybir.AxisListType
F32 = mybir.dt.float32
BF16 = mybir.dt.bfloat16
I32 = mybir.dt.int32
U32 = mybir.dt.uint32

P = 128
SEQS, SEQ, D = 8, 256, 256
TOKENS = SEQS * SEQ
TILES = TOKENS // P
KD = D // P
HEADS, HD = 16, 16
GROUPS = 4
HALVES = 2
HT = TILES // HALVES
HS = SEQS // HALVES
HTOK = TOKENS // HALVES
CHUNK = 512
CHUNKS = HTOK // CHUNK
CT = CHUNK // P
QT = SEQ // P
VW = HD + 1
PARTS = 3
STACK = 6 * HD
ROWS = STACK + 2
Q_PARTS = (0, 0, 1, 1, 0, 2)
K_PARTS = (0, 1, 0, 1, 2, 0)
EPS = 1e-5
NSEL, SELW, LORA = 8, 8, 8
FW = NSEL * SELW + NSEL + NSEL * LORA
MW = NSEL * LORA + NSEL
EXPERTS, INNER, TOPK = 32, 128, 4
MASKED = -1.0e30
BLOCKS = -(-(TOKENS * TOPK + EXPERTS * (P - 1)) // P)
BLOCKS += -BLOCKS % 4
FEWEST = TOKENS * TOPK // P // 4
EW = 2 * KD * INNER + D
CLAMP = 7.0
P_RING = 4
LAG = 3
JOB_BANKS = 5

JOBS0 = [(c, kind) for c in range(CHUNKS) for kind in ("T0", "T1", "Q0", "Q1", "K0", "K1", "V0", "V1")]
JOBS1 = [(c, kind) for c in range(CHUNKS) for kind in ("T0", "T1", "Q0", "Q1", "K0", "V0")]
SPLIT0 = [j for j in JOBS0 if j[1][0] in "QK"]
SPLIT1 = [j for j in JOBS1 if j[1][0] in "QK"]
FFN_JOBS = 2 * CHUNKS + HT // 2 + CHUNKS + HT // 2
JOB_F = 2 * CHUNKS + HT // 2
JOB_1 = JOB_F + FFN_JOBS

TURN = 6
RING_USES = []
for _b in range(HS):
    for _s in range(HEADS):
        RING_USES.append((_b, _s))
        if _b and _s == TURN:
            RING_USES += [(_b - 1, HEADS + _q) for _q in range(QT)]
RING_USES += [(HS - 1, HEADS + _q) for _q in range(QT)]


def ring_use(layer, b, s):
    return RING_USES.index((b, s))


UNITS = (
    [(qt, h, 2, SEQ) for h in range(0, HEADS, 2) for qt in range(QT)],
    [(0, h, 4, P) for h in range(0, HEADS, 4)] + [(1, h, 2, SEQ) for h in range(0, HEADS, 2)],
)
DVE_STEPS = (15, 32)


def heads_of_kv(layer, h):
    return h if layer == 0 else h // (HEADS // GROUPS)


def two_block_kernel(nc, x_in, wqkv0, wproj, bproj, wffn, debias, wdown, center, slope,
                     wqkv1, bq1, bk1, bv1, router, ebias, wexp_in, out):
    ctx = ExitStack()
    with ctx:
        def sb(name, shape, dt=F32):
            return ctx.enter_context(nc.sbuf_tensor(name, shape, dt))

        def sem(name):
            return ctx.enter_context(nc.semaphore(name))

        def cut(whole, start, size, shape=None, **axes):
            part = whole[:, start:start + size]
            return part.rearrange(shape, **axes) if shape else part

        x = sb("x", [P, TILES, D])
        norms = sb("norms", [P, TILES * D])
        xn = cut(norms, 0, HT * D, "p (t d) -> p t d", t=HT)
        xnT = cut(norms, HT * D, KD * HTOK, "p (k t) -> p k t", k=KD)
        xnT4 = cut(norms, 0, KD * TOKENS, "p (k t) -> p k t", k=KD)
        attn_w = sb("attn_w", [P, KD * (3 * D + D + D + 2 * GROUPS * HD)])
        w0 = cut(attn_w, 0, KD * 3 * D, "p (k n) -> p k n", k=KD)
        wp = cut(attn_w, KD * 3 * D, KD * D, "p (k n) -> p k n", k=KD)
        w1 = cut(attn_w, KD * 4 * D, KD * (D + 2 * GROUPS * HD), "p (k n) -> p k n", k=KD)
        xbT = cut(attn_w, 2 * D, 2 * D, "p (b k t) -> p b k t", b=2, k=KD)
        gu = cut(attn_w, 4 * D, 4 * INNER, "p (b g i) -> p b g i", b=2, g=2)
        ge = cut(attn_w, 6 * D, 2 * INNER, "p (b i) -> p b i", b=2)
        hid = cut(attn_w, 6 * D + 2 * INNER, 2 * INNER, "p (b i) -> p b i", b=2)
        yb = cut(attn_w, 6 * D + 6 * INNER, 2 * D, "p (b d) -> p b d", b=2)
        ffn_w = sb("ffn_w", [P, KD * FW])
        wf = cut(ffn_w, 0, KD * FW, "p (k f) -> p k f", k=KD)
        wdb = sb("wdb", [P, KD, NSEL])
        wd_all = sb("wd", [P, D])
        wd = wd_all[0:MW, :]
        bpb = sb("bpb", [P, D])
        bq = sb("bq", [P, KD])
        bk = sb("bk", [GROUPS * HD, 1])
        bvb = sb("bvb", [P, GROUPS * HD])
        cenb = sb("cenb", [P, NSEL])
        slob = sb("slob", [P, NSEL])
        ident = sb("ident", [P, P])
        identb = sb("identb", [P, P], BF16)
        ones = sb("ones", [P, P])
        mask_s = sb("mask_s", [P, P], BF16)
        mask_t = sb("mask_t", [P, P], BF16)
        iota8 = sb("iota8", [P, NSEL])
        products = sb("products", [P, KD * FW])
        prod = cut(products, 0, KD * FW, "p (k f) -> p k f", k=KD)
        constb = sb("constb", [P, FW])
        sizes = [HEADS * HTOK // 2, HT * HEADS * VW, SEQS * QT * HEADS * HD, HEADS * HTOK // 2,
                 GROUPS * HTOK // 2, HT * GROUPS * VW]
        at = [sum(sizes[:i]) for i in range(len(sizes) + 1)]
        arena = sb("arena", [P, max(at[-1], EXPERTS * EW)])
        stack = "p (h t) -> p h t"
        ks = [cut(arena, at[0], sizes[0]).bitcast(BF16).rearrange(stack, h=HEADS)[0:ROWS],
              cut(arena, at[4], sizes[4]).bitcast(BF16).rearrange(stack, h=GROUPS)[0:ROWS]]
        qs = cut(arena, at[3], sizes[3]).bitcast(BF16).rearrange(stack, h=HEADS)[0:ROWS]
        v = [cut(arena, at[1], sizes[1], "p (t h w) -> p t h w", t=HT, h=HEADS),
             cut(arena, at[5], sizes[5], "p (t h w) -> p t h w", t=HT, h=GROUPS)]
        splits = sb("splits", [P, 4 * PARTS * CHUNK // 2 + 4 * CHUNK])
        parts = cut(splits, 0, 4 * PARTS * CHUNK // 2).bitcast(BF16).rearrange(
            "p (s a t) -> p s a t", s=4, a=PARTS)
        rest = cut(splits, 4 * PARTS * CHUNK // 2, 4 * CHUNK, "p (s t) -> p s t", s=4)
        xn4 = cut(splits, 0, TILES * D, "p (t d) -> p t d", t=TILES)
        te = TILES * EXPERTS
        tile_expert = "p (t e) -> p t e"
        lg = cut(splits, TILES * D, te, tile_expert, t=TILES)
        sp1 = cut(splits, TILES * D + te, te, tile_expert, t=TILES)
        exps = sb("exps", [P, P_RING * 2 * SEQ])
        pt = cut(exps, 0, P_RING * 2 * SEQ, "p (r t) -> p r t", r=P_RING)
        work = cut(exps, 0, TILES * TOPK * EXPERTS, "p (t k e) -> p t k e", t=TILES, k=TOPK)
        pick = sb("pick", [P, TILES, TOPK, EXPERTS])
        mx = sb("mx", [P, QT, HEADS])
        neg = sb("neg", [P, QT, 2, HEADS], BF16)
        negT = sb("negT", [2 * HEADS, SEQ], BF16)
        rec = sb("rec", [P, QT, HEADS])
        rowbuf = sb("rowbuf", [P, QT * D + HT * FW + HT * NSEL * SELW + HT * MW])
        pvs = cut(norms, 0, 4 * SEQ, "p (g q) -> p g q", g=4)
        att = cut(rowbuf, 0, QT * D, "p (q d) -> p q d", q=QT)
        ctx0 = cut(arena, at[2], sizes[2], "p (j q h d) -> p j q h d", j=SEQS, q=QT, h=HEADS)
        st = sb("st", [P, TILES, 6])
        mv = sb("mv", [P, TILES, 2])
        var = sb("var", [P, TILES])
        sd = sb("sd", [P, TILES])
        rstd = sb("rstd", [P, TILES])
        g = cut(rowbuf, QT * D, HT * FW, "p (t f) -> p t f", t=HT)
        sq = cut(rowbuf, QT * D + HT * FW, HT * NSEL * SELW, "p (t f) -> p t f", t=HT)
        xx = sb("xx", [P, HT])
        sc = [sb(f"sc{i}", [P, HT, NSEL]) for i in range(4)]
        top = sb("top", [P, HT])
        least = sb("least", [P, HT])
        keep = sb("keep", [P, HT])
        mm = cut(rowbuf, QT * D + HT * FW + HT * NSEL * SELW, HT * MW, "p (t f) -> p t f", t=HT)
        sg, su, se, sh = (cut(rowbuf, i * CHUNK, CHUNK) for i in range(4))
        slots_e = cut(rowbuf, 4 * CHUNK, te, tile_expert, t=TILES)
        turned_m = sb("turned_m", [P, HTOK])
        mT = turned_m[0:MW, :]
        sco = cut(turned_m, 0, te, tile_expert, t=TILES)
        sbi = cut(turned_m, te, te, tile_expert, t=TILES)
        xb = cut(turned_m, 0, 4 * D, "p (b d) -> p b d", b=4)
        wr = sb("wr", [P, KD, EXPERTS])
        wsh = sb("wsh", [P, EW])
        ebb = sb("ebb", [P, EXPERTS])
        iota32 = sb("iota32", [P, EXPERTS])
        iota_b = sb("iota_b", [1, BLOCKS])
        zero = sb("zero", [P, 64])
        before = sb("before", [P, P], BF16)
        onesb = sb("onesb", [P, P], BF16)
        m8 = cut(ffn_w, 0, TILES * 8, "p (t e) -> p t e", t=TILES)
        i8 = cut(ffn_w, TILES * 8, TILES * 8).bitcast(U32).rearrange("p (t e) -> p t e", t=TILES)
        pk = [sb(f"pk{i}", [P, TILES, TOPK]) for i in range(2)]
        ps = [sb(f"ps{i}", [P, TILES]) for i in range(2)]
        chosen = cut(products, 0, te // 2).bitcast(BF16).rearrange(tile_expert, t=TILES)
        cnt = [cut(wd_all, i * EXPERTS, EXPERTS) for i in range(4)]
        eb_f = wd_all[0:1, 4 * EXPERTS:4 * EXPERTS + BLOCKS]
        cnti = [cut(bpb, i * EXPERTS, EXPERTS).bitcast(I32) for i in range(2)]
        slot = cut(bpb, 2 * EXPERTS, TILES * TOPK).bitcast(U32).rearrange("p (t k) -> p t k", t=TILES)
        eb_i = sb("eb_i", [1, BLOCKS], I32)
        wgu = cut(norms, 0, 4 * KD * INNER, "p (b w) -> p b w", b=2)
        hold = sb("hold", [1, 2], F32)
        trips_i = sb("trips_i", [1, 2], I32)
        YG = 8
        yg = cut(arena, 0, YG * D, "p (r d) -> p r d", r=YG)

        bank = [ctx.enter_context(nc.psum_tensor(f"bank{i}", [P, 512], F32)) for i in range(8)]
        unit_bank, st_bank, pv_bank, misc = bank[0:2], bank[2:5], bank[5:7], bank[7]

        scratch = [nc.dram_tensor(f"parts_dram{n}", [CHUNKS, PARTS, c, CHUNK], BF16, kind="Internal").ap()
                   for n, c in ((0, 2 * D), (1, D + GROUPS * HD))]
        xs = nc.dram_tensor("rows_by_expert", [BLOCKS * P, D], F32, kind="Internal").ap()
        ys = nc.dram_tensor("results_by_expert", [BLOCKS * P, D], F32, kind="Internal").ap()

        weights_loaded = sem("weights_loaded")
        x_loaded = sem("x_loaded")
        constants_made = sem("constants_made")
        pool_step = sem("pool_step")
        products_made = sem("products_made")
        sums_made = sem("sums_made")
        sums_copied = sem("sums_copied")
        dve_step = [sem(f"dve_step{n}") for n in range(2)]
        act_step = sem("act_step")
        var_ready = [sem(f"var_ready{n}") for n in range(2)]
        sd_ready = [sem(f"sd_ready{n}") for n in range(2)]
        xn_ready = [sem(f"xn_ready{n}") for n in range(2)]
        bias_added = sem("bias_added")
        rows_moved = sem("rows_moved")
        job_ready = [sem(f"job_ready{n}") for n in range(2)]
        job_done = [sem(f"job_done{n}") for n in range(2)]
        hi_ready = [sem(f"hi_ready{n}") for n in range(2)]
        mid_ready = [sem(f"mid_ready{n}") for n in range(2)]
        low_ready = [sem(f"low_ready{n}") for n in range(2)]
        saved = [[sem(f"saved{n}_{i}") for i in range(4)] for n in range(2)]
        stacked = [[sem(f"stacked{n}_{c}") for c in range(CHUNKS)] for n in range(2)]
        unit_ready = [sem(f"unit_ready{n}") for n in range(2)]
        unit_done = [sem(f"unit_done{n}") for n in range(2)]
        neg_ready = [sem(f"neg_ready{n}") for n in range(2)]
        negT_ready = [sem(f"negT_ready{n}") for n in range(2)]
        negT_copied = [sem(f"negT_copied{n}") for n in range(2)]
        neg_stacked = [sem(f"neg_stacked{n}") for n in range(2)]
        st_ready = [sem(f"st_ready{n}") for n in range(2)]
        exp_ready = [sem(f"exp_ready{n}") for n in range(2)]
        pv_ready = [sem(f"pv_ready{n}") for n in range(2)]
        squares_ready = sem("squares_ready")
        logit_ready = sem("logit_ready")
        gate_exp_ready = sem("gate_exp_ready")
        selected = sem("selected")
        out_done = sem("out_done")
        xs_cleared = sem("xs_cleared")
        ys_cleared = sem("ys_cleared")
        ones_placed = sem("ones_placed")
        qkv_loaded = sem("qkv_loaded")
        pvs_ready = [sem(f"pvs_ready{n}") for n in range(2)]
        divided = [sem(f"divided{n}") for n in range(2)]
        turned_back = [sem(f"turned_back{n}") for n in range(2)]
        experts_loaded = sem("experts_loaded")
        xn4_ready = sem("xn4_ready")
        var4_ready = sem("var4_ready")
        sd4_ready = sem("sd4_ready")
        turn4_ready = sem("turn4_ready")
        turn4_copied = sem("turn4_copied")
        logits_ready = sem("logits_ready")
        route_ready = sem("route_ready")
        route_act = sem("route_act")
        chosen_ready = sem("chosen_ready")
        ranks_ready = sem("ranks_ready")
        slots_ready = sem("slots_ready")
        blocks_ready = sem("blocks_ready")
        scattered = sem("scattered")
        moe_step = sem("moe_step")
        sgu_ready = sem("sgu_ready")
        sgu_clipped = sem("sgu_clipped")
        stanh_ready = sem("stanh_ready")
        shid_ready = sem("shid_ready")
        sdown_ready = sem("sdown_ready")
        sdown_added = sem("sdown_added")
        xb_loaded = [sem(f"xb_loaded{i}") for i in range(4)]
        xb_turned = sem("xb_turned")
        xbT_copied = sem("xbT_copied")
        gu_ready = sem("gu_ready")
        gu_clipped = sem("gu_clipped")
        ge_ready = sem("ge_ready")
        hid_step = sem("hid_step")
        staged = sem("staged")
        hid_ready = sem("hid_ready")
        y_ready = sem("y_ready")
        yb_copied = sem("yb_copied")
        all_stored = sem("all_stored")
        y_stored = [sem(f"y_stored{i}") for i in range(2)]
        gathered = [sem(f"gathered{i}") for i in range(8)]
        y_added = sem("y_added")

        RING = (4, 3)
        SPLITS = (SPLIT0, SPLIT1)
        LAYER_JOBS = (JOBS0, JOBS1)
        JOB0 = (0, JOB_1)
        JOBS = (len(JOBS0), JOB_1 + len(JOBS1))
        NORMS = (1, 2)
        QK_ROWS = (2 * D, D + GROUPS * HD)

        def pair_of(b, p):
            return b // 2 if isinstance(b, int) else (b - p) // 2

        def block_trips(eng):
            eng.wait_ge(blocks_ready, 1)
            return eng.value_load(trips_i[0:1, 1:2], min_val=0, max_val=BLOCKS // 4 - FEWEST) + FEWEST

        def wide(row, n):
            return row.broadcast_to([P, n])

        def halves(w):
            return w.rearrange("(k p) n -> p k n", p=P)

        CONSTANTS = 13
        WEIGHTS = [
            (wf[:, :, :], halves(wffn)), (wdb[:, :, :], halves(debias)), 
            (wp[:, :, :], halves(wproj)), (wd, wdown), (bpb[:, :], wide(bproj, D)),
            (cenb[:, :], wide(center, NSEL)), (slob[:, :], wide(slope, NSEL)),
            (wr[:, :, :], halves(router)), (ebb[:, :], wide(ebias, EXPERTS)), (wsh[:, :], wexp_in[:, EXPERTS, :]),
            (w1[:, :, :], halves(wqkv1)), (bq[:, :], bq1), (bk[:, :], bk1), (bvb[:, :], wide(bv1, GROUPS * HD)),
        ]

        block = ctx.enter_context(nc.Block())

        @block.sync
        def _(sp):
            xr = x_in.rearrange("(t p) d -> p t d", p=P)
            sp.dma_start(x[:, 0:HT, :], xr[:, 0:HT, :]).then_inc(x_loaded, 16)
            sp.dma_start(w0[:, :, :], halves(wqkv0)).then_inc(qkv_loaded, 16)
            for dst, src in WEIGHTS:
                sp.dma_start(dst, src).then_inc(weights_loaded, 16)
            sp.wait_ge(x_loaded, 16)
            sp.dma_start(x[:, HT:TILES, :], xr[:, HT:TILES, :]).then_inc(x_loaded, 16)

            sp.wait_ge(constants_made, CONSTANTS)
            for n, kv in ((0, HEADS), (1, GROUPS)):
                rows = kv * HTOK // P
                for r in range(STACK, ROWS):
                    sp.dma_start(ks[n][r:r + 1, :, :], onesb[0:rows, :]).then_inc(ones_placed, 16)

            def restack(half, n):
                kv = HEADS if n == 0 else GROUPS
                per_chunk = len(SPLITS[n]) // CHUNKS
                for c in range(CHUNKS):
                    for i in range(per_chunk):
                        j = c * per_chunk + i
                        slot = j % RING[n]
                        rows = min(P, QK_ROWS[n] - i * P)
                        sp.wait_ge(low_ready[n], half * len(SPLITS[n]) + j + 1)
                        sp.dma_start(scratch[n][c, :, i * P:i * P + rows, :].rearrange("a r t -> r a t"),
                                     parts[0:rows, slot, :, :]).then_inc(saved[n][slot], 16)
                    for slot in range(RING[n]):
                        uses = len([j for j in range(len(SPLITS[n])) if j % RING[n] == slot])
                        upto = len([j for j in range((c + 1) * per_chunk) if j % RING[n] == slot])
                        sp.wait_ge(saved[n][slot], (half * uses + upto) * 16)
                    at = slice(c * CHUNK, (c + 1) * CHUNK)
                    for blk in range(6):
                        rows = slice(blk * HD, (blk + 1) * HD)
                        sp.dma_start(qs[rows, :, at],
                                     scratch[n][c, Q_PARTS[blk], 0:D, :].rearrange("(h d) t -> d h t", d=HD)
                                     ).then_inc(stacked[n][c], 16)
                        sp.dma_start(ks[n][rows, :, at],
                                     scratch[n][c, K_PARTS[blk], D:D + kv * HD, :]
                                     .rearrange("(h d) t -> d h t", d=HD)).then_inc(stacked[n][c], 16)

            def stack_maxima(half, n):
                for b in range(HS):
                    sp.wait_ge(negT_copied[n], half * HS + b + 1)
                    for part in range(2):
                        sp.dma_start(qs[STACK + part:STACK + part + 1, :, b * SEQ:(b + 1) * SEQ],
                                     negT[part * HEADS:(part + 1) * HEADS, :]).then_inc(neg_stacked[n], 16)

            for half in range(HALVES):
                restack(half, 0)
                stack_maxima(half, 0)
            sp.dma_start(xs.rearrange("(p r) (a c) -> p (r a) c", p=P, c=64),
                         zero[:, :].unsqueeze(1).broadcast_to([P, BLOCKS * D // 64, 64])).then_inc(xs_cleared, 16)
            unused = ys[4 * FEWEST * P:BLOCKS * P, :]
            sp.dma_start(unused.rearrange("(p r) (a c) -> p (r a) c", p=P, c=64),
                         zero[:, :].unsqueeze(1).broadcast_to([P, (BLOCKS - 4 * FEWEST) * D // 64, 64])
                         ).then_inc(ys_cleared, 16)
            for half in range(HALVES):
                restack(half, 1)
                stack_maxima(half, 1)
            sp.wait_ge(divided[1], SEQS * QT)
            sp.dma_start(arena[:, 0:EXPERTS * EW].rearrange("p (e w) -> p e w", e=EXPERTS),
                         wexp_in[:, 0:EXPERTS, :]).then_inc(experts_loaded, 16)
            sp.wait_ge(scattered, TILES * TOPK * 16)

            def load_block(b, i, p, again):
                if again:
                    sp.wait_ge(xb_turned, b - 3)
                sp.dma_start(xb[:, p, :], xs[bass.ds(b * P, P), :]).then_inc(xb_loaded[p], 16)

            for b in range(8):
                load_block(b, b // 4, b % 4, b >= 4)
            with sp.Fori(2, block_trips(sp)) as i:
                for j in range(4):
                    load_block(4 * i + j, i, j, True)
            outr = out.rearrange("(t p) d -> p t d", p=P)
            for t in range(0, TILES, 2):
                sp.wait_ge(y_added, (t + 2) * TOPK)
                sp.dma_start(outr[:, t:t + 2, :], x[:, t:t + 2, :]).then_inc(out_done, 16)
            sp.wait_ge(out_done, TILES // 2 * 16)

        @block.gpsimd
        def _(pool):
            pool.memset(ident[:, :], 0.0).then_inc(pool_step, 1)
            pool.memset(mask_s[:, :], 0.0).then_inc(pool_step, 1)
            pool.memset(mask_t[:, :], 0.0).then_inc(pool_step, 1)
            pool.memset(before[:, :], 1.0).then_inc(pool_step, 1)
            pool.memset(onesb[:, :], 1.0).then_inc(constants_made, 1)
            pool.memset(zero[:, :], 0.0).then_inc(constants_made, 1)
            pool.iota(iota32[:, :], [[1, EXPERTS]], base=0, channel_multiplier=0,
                      allow_small_or_imprecise_dtypes=True).then_inc(constants_made, 1)
            pool.memset(ones[:, :], 1.0).then_inc(constants_made, 1)
            for n in range(2):
                pool.memset(v[n][:, :, :, HD:VW], 1.0).then_inc(constants_made, 1)
            pool.iota(iota8[:, :], [[1, NSEL]], base=0, channel_multiplier=0,
                      allow_small_or_imprecise_dtypes=True).then_inc(constants_made, 1)
            pool.wait_ge(pool_step, 4)
            pool.affine_select(out=ident[:, :], in_=ident[:, :], compare_op=ALU.not_equal, fill=1.0, base=0,
                               pattern=[[-1, P]], channel_multiplier=1).then_inc(pool_step, 1)
            pool.affine_select(out=mask_s[:, :], in_=mask_s[:, :], compare_op=ALU.is_ge, fill=MASKED, base=0,
                               pattern=[[-1, P]], channel_multiplier=1).then_inc(constants_made, 1)
            pool.affine_select(out=mask_t[:, :], in_=mask_t[:, :], compare_op=ALU.is_ge, fill=MASKED, base=0,
                               pattern=[[1, P]], channel_multiplier=-1).then_inc(constants_made, 1)
            pool.affine_select(out=before[:, :], in_=before[:, :], compare_op=ALU.is_gt, fill=0.0, base=0,
                               pattern=[[1, P]], channel_multiplier=-1).then_inc(constants_made, 1)
            pool.wait_ge(pool_step, 5)
            pool.tensor_copy(identb[:, :], ident[:, :]).then_inc(constants_made, 1)

            def low_parts(half, n):
                for j, (c, kind) in enumerate(SPLITS[n]):
                    rows = GROUPS * HD if n == 1 and kind == "K0" else P
                    slot = j % RING[n]
                    pool.wait_ge(mid_ready[n], half * len(SPLITS[n]) + j + 1)
                    if rows < P:
                        pool.wait_ge(low_ready[n], half * len(SPLITS[n]) + j)
                    pool.tensor_tensor(parts[0:rows, slot, 2, :], rest[0:rows, slot, :],
                                       parts[0:rows, slot, 1, :], ALU.subtract).then_inc(low_ready[n], 1)

            for half in range(HALVES):
                low_parts(half, 0)
                pool.wait_ge(weights_loaded, 16 * len(WEIGHTS))
                pool.wait_ge(xn_ready[0], (half + 1) * HT)
                pool.tensor_tensor(x[:, bass.ds(half * HT, HT), :], x[:, bass.ds(half * HT, HT), :],
                                   bpb[:, :].unsqueeze(1).broadcast_to([P, HT, D]), ALU.add).then_inc(bias_added, 1)
            for half in range(HALVES):
                low_parts(half, 1)
            pool.iota(iota_b[:, :], [[1, BLOCKS]], base=0, channel_multiplier=0,
                      allow_small_or_imprecise_dtypes=True).then_inc(pool_step, 1)
            pool.wait_ge(xs_cleared, 16)
            pool.wait_ge(slots_ready, 1)
            for t in range(TILES):
                for k in range(TOPK):
                    pool.indirect_dma_start(xs, bass.IndirectOffsetOnAxis(ap=slot[:, t, k:k + 1], axis=0),
                                            xn4[:, t, :], None).then_inc(scattered, 16)
            pool.wait_ge(all_stored, 2)
            for n in range(TILES * TOPK):
                t, k = divmod(n, TOPK)
                if n >= YG:
                    pool.wait_ge(y_added, n - YG + 1)
                pool.indirect_dma_start(yg[:, n % YG, :], None, ys,
                                        bass.IndirectOffsetOnAxis(ap=slot[:, t, k:k + 1], axis=0)
                                        ).then_inc(gathered[n % YG], 16)

        @block.scalar
        def _(act):
            def deviation(half, n, k):
                act.wait_ge(var_ready[n], half * NORMS[n] + k + 1)
                act.activation(sd[:, 0:HT], var[:, 0:HT], ACT.Sqrt).then_inc(sd_ready[n], 1)

            def split(half, n):
                count = len(SPLITS[n])

                def middle(j):
                    rows = GROUPS * HD if n == 1 and SPLITS[n][j][1] == "K0" else P
                    job = JOB0[n] + LAYER_JOBS[n].index(SPLITS[n][j])
                    act.wait_ge(job_done[n], half * JOBS[n] + job + 1)
                    act.activation(parts[0:rows, j % RING[n], 1, :], rest[0:rows, j % RING[n], :],
                                   ACT.Copy).then_inc(mid_ready[n], 1)

                for j, (c, kind) in enumerate(SPLITS[n]):
                    slot = j % RING[n]
                    uses = len([i for i in range(count) if i % RING[n] == slot])
                    before = len([i for i in range(j) if i % RING[n] == slot])
                    job = LAYER_JOBS[n].index((c, kind))
                    if j >= RING[n]:
                        act.wait_ge(saved[n][slot], (half * uses + before) * 16)
                    act.wait_ge(job_ready[n], half * JOBS[n] + JOB0[n] + job + 1)
                    src = bank[(JOB0[n] + job) % JOB_BANKS]
                    if n == 0:
                        ins = act.activation(parts[:, slot, 0, :], src[:, :], ACT.Copy)
                    elif kind == "K0":
                        ins = act.activation(parts[0:GROUPS * HD, slot, 0, :], src[0:GROUPS * HD, :],
                                             ACT.Identity, bias=bk[:, :])
                    else:
                        m = int(kind[1])
                        ins = act.activation(parts[:, slot, 0, :], src[:, :], ACT.Identity, bias=bq[:, m:m + 1])
                    ins.then_inc(hi_ready[n], 1)
                    if j >= 1:
                        middle(j - 1)
                middle(count - 1)

            def copy_maxima(half, n, b):
                act.wait_ge(negT_ready[n], half * HS + b + 1)
                act.activation(negT[:, :], misc[0:2 * HEADS, 0:SEQ // 2].bitcast(BF16), ACT.Copy
                               ).then_inc(negT_copied[n], 1)

            def copy_sums(half, n, b, k):
                act.wait_ge(pv_ready[n], (half * HS + b) * HEADS + 8 * (k + 1))
                if b > 0 or half > 0:
                    act.wait_ge(turned_back[n], (half * HS + b) * QT)
                act.activation(pvs[:, 2 * k:2 * k + 2, :].rearrange("p g q -> p (g q)"), pv_bank[k][:, :], ACT.Copy
                               ).then_inc(pvs_ready[n], 1)

            def attention(half, n):
                width = 2 * SEQ if n == 0 else SEQ + P
                copy_maxima(half, n, 0)
                for b in range(HS):
                    for s in range(HEADS):
                        i = b * HEADS + s
                        act.wait_ge(st_ready[n], half * HS * HEADS + i + 1)
                        if i >= P_RING:
                            act.wait_ge(pv_ready[n], half * HS * HEADS + i - P_RING + 1)
                        act.activation(pt[:, i % P_RING, 0:width], st_bank[ring_use(n, b, s) % 3][:, 0:width], ACT.Exp,
                                       scale=HD ** -0.5).then_inc(exp_ready[n], 1)
                        if s == 11 and b + 1 < HS:
                            copy_maxima(half, n, b + 1)
                        if s == 8 + LAG:
                            copy_sums(half, n, b, 0)
                        if b > 0 and s == LAG:
                            copy_sums(half, n, b - 1, 1)
                copy_sums(half, n, HS - 1, 1)

            for half in range(HALVES):
                deviation(half, 0, 0)
                split(half, 0)
                attention(half, 0)
            act.wait_ge(weights_loaded, 16 * len(WEIGHTS))
            for half in range(HALVES):
                deviation(half, 1, 0)
                for t in range(HT):
                    act.wait_ge(xn_ready[1], half * 2 * HT + t + 1)
                    act.activation(pt[:, 0, 0:D], xn[:, t, :], ACT.Square,
                                   accum_out=xx[:, t:t + 1]).then_inc(squares_ready, 1)
                    act.wait_ge(squares_ready, half * HT + t + 1)
                act.wait_ge(logit_ready, half + 1)
                act.activation(sc[1][:, :, :], sc[0][:, :, :], ACT.Exp, scale=-1.0).then_inc(gate_exp_ready, 1)
                deviation(half, 1, 1)
                split(half, 1)
                attention(half, 1)
            act.wait_ge(var4_ready, 1)
            act.activation(sd[:, :], var[:, :], ACT.Sqrt).then_inc(sd4_ready, 1)
            act.wait_ge(route_ready, 1)
            act.activation(sbi, sp1, ACT.Exp).then_inc(route_act, 1)
            act.wait_ge(route_ready, 2)
            act.activation(sp1, sbi, ACT.Ln).then_inc(route_act, 1)
            act.wait_ge(route_ready, 3)
            act.activation(sco, sbi, ACT.Sqrt).then_inc(route_act, 1)
            for c in range(TOKENS // CHUNK):
                act.wait_ge(sgu_clipped, c + 1)
                act.activation(se, sg, ACT.Tanh, scale=0.5).then_inc(stanh_ready, 1)

            def copy_xbT(b, p):
                act.wait_ge(xb_turned, b + 1)
                act.activation(xbT[:, p, :, :].rearrange("p k t -> p (k t)"), bank[p][:, 0:D], ACT.Copy
                               ).then_inc(xbT_copied, 1)

            def gate_tanh(b, p):
                act.wait_ge(gu_clipped, b + 1)
                act.activation(ge[:, p, :], gu[:, p, 0, :], ACT.Tanh, scale=0.5).then_inc(ge_ready, 1)

            act.wait_ge(ys_cleared, 16)

            def store_y(b, p, again):
                act.wait_ge(y_ready, b + 1)
                if again:
                    act.wait_ge(y_stored[p], pair_of(b, p) * 16)
                act.activation(yb[:, p, :], bank[6 + p][:, 0:D], ACT.Copy).then_inc(yb_copied, 1)
                act.wait_ge(yb_copied, b + 1)
                act.dma_start(ys[bass.ds(b * P, P), :], yb[:, p, :]).then_inc(y_stored[p], 16)

            def act_step(s, p, first=8):
                copy_xbT(s, p)
                if first >= 1:
                    gate_tanh(s - 1, 1 - p)
                if first >= 3:
                    store_y(s - 3, 1 - p, first >= 5)

            for s in range(8):
                act_step(s, s % 2, s)
            trips = block_trips(act)
            with act.Fori(2, trips) as i:
                for j in range(4):
                    act_step(4 * i + j, j % 2)
            end = trips * 4
            gate_tanh(end - 1, 1)
            for j in range(3):
                store_y(end - 3 + j, (1 + j) % 2, True)

        @block.tensor
        def _(pe):
            pe.wait_ge(constants_made, CONSTANTS)
            pe.wait_ge(ones_placed, 64)
            pe.wait_ge(qkv_loaded, 16)

            def transposes(half, n, job, norm, c, k):
                pe.wait_ge(xn_ready[n], half * NORMS[n] * HT + norm * HT + (c + 1) * CT)
                for t in range(CT):
                    ins = pe.transpose(bank[job % JOB_BANKS][:, t * P:(t + 1) * P],
                                       xn[:, c * CT + t, k * P:(k + 1) * P], ident[:, :])
                ins.then_inc(job_ready[n], 1)

            def bank_free(half, n, job, first):
                if job - first >= JOB_BANKS:
                    pe.wait_ge(job_done[n], half * JOBS[n] + job - JOB_BANKS + 1)

            def project(half, n):
                w = (w0, w1)[n]
                kv = HEADS if n == 0 else GROUPS
                for i, (c, kind) in enumerate(LAYER_JOBS[n]):
                    job = JOB0[n] + i
                    b = bank[job % JOB_BANKS]
                    bank_free(half, n, job, JOB0[n])
                    at = slice(c * CHUNK, (c + 1) * CHUNK)
                    if kind[0] == "T":
                        transposes(half, n, job, n, c, int(kind[1]))
                        continue
                    if kind == "Q0":
                        pe.wait_ge(job_done[n], half * JOBS[n] + job)
                    if kind[0] in "QK":
                        col = (D if kind[0] == "K" else 0) + int(kind[1]) * P
                        rows = GROUPS * HD if n == 1 and kind == "K0" else P
                        for k in range(KD):
                            ins = pe.matmul(b[0:rows, :], w[:, k, col:col + rows], xnT[:, k, at],
                                            start=(k == 0), stop=(k == KD - 1))
                    else:
                        width = kv * HD
                        per = 512 // width if n == 0 else CT
                        for t in range(per):
                            tok = c * CHUNK + (int(kind[1]) * per + t) * P
                            for k in range(KD):
                                ins = pe.matmul(b[:, t * width:(t + 1) * width], xnT[:, k, tok:tok + P],
                                                w[:, k, D + width:D + 2 * width],
                                                start=(k == 0), stop=(k == KD - 1))
                    ins.then_inc(job_ready[n], 1)

            def unit(half, n, b, u):
                qt, h0, nh, nk = UNITS[n][u]
                i = b * len(UNITS[n]) + u
                if i >= 2:
                    pe.wait_ge(unit_done[n], half * HS * len(UNITS[n]) + i - 1)
                dst = unit_bank[i % 2]
                for a in range(nh):
                    ins = pe.matmul(dst[:, a * nk:(a + 1) * nk],
                                    qs[0:STACK, h0 + a, b * SEQ + qt * P:b * SEQ + (qt + 1) * P],
                                    ks[n][0:STACK, heads_of_kv(n, h0 + a), b * SEQ:b * SEQ + nk],
                                    start=True, stop=(n == 0))
                    if n == 1:
                        ins = pe.matmul(dst[:, a * nk + nk - P:(a + 1) * nk], identb[:, :], mask_s[:, :],
                                        start=False, stop=True)
                ins.then_inc(unit_ready[n], 1)

            def turn_maxima(half, n, b):
                pe.wait_ge(neg_ready[n], half * HS + b + 1)
                for qt in range(QT):
                    ins = pe.transpose(misc[0:2 * HEADS, qt * P // 2:(qt + 1) * P // 2].bitcast(BF16),
                                       neg[:, qt, :, :].rearrange("p a h -> p (a h)"), identb[:, :])
                ins.then_inc(negT_ready[n], 1)

            def wait_ring(half, n, r):
                if r < 3:
                    return
                b, s = RING_USES[r - 3]
                if s < HEADS:
                    pe.wait_ge(exp_ready[n], half * HS * HEADS + b * HEADS + s + 1)
                else:
                    pe.wait_ge(divided[n], (half * HS + b) * 2 + s - HEADS + 1)

            def scores(half, n, b, s):
                i = b * HEADS + s
                r = ring_use(n, b, s)
                wait_ring(half, n, r)
                dst = st_bank[r % 3]
                kh = heads_of_kv(n, s)
                for kt in range(QT):
                    keys = ks[n][0:ROWS, kh, b * SEQ + kt * P:b * SEQ + (kt + 1) * P]
                    q0 = 0 if n == 0 or kt == 0 else P
                    at = kt * SEQ
                    ins = pe.matmul(dst[:, at:at + SEQ - q0], keys, qs[0:ROWS, s, b * SEQ + q0:(b + 1) * SEQ],
                                    start=True, stop=(n == 0))
                    if n == 1:
                        ins = pe.matmul(dst[:, at:at + P], identb[:, :], mask_t[:, :], start=False, stop=True)
                ins.then_inc(st_ready[n], 1)

            def values(half, n, i):
                b, h = divmod(i, HEADS)
                pe.wait_ge(exp_ready[n], half * HS * HEADS + i + 1)
                if h % 8 == 0 and half * HS + b:
                    pe.wait_ge(pvs_ready[n], (half * HS + b) * 2 - 1 + h // 8)
                p = pt[:, i % P_RING, :]
                kh = heads_of_kv(n, h)
                half_bank = 8 * (h // 8)
                rows = slice(h % 4 * 32, h % 4 * 32 + VW)
                col = (h - half_bank) // 4 * SEQ
                dst = pv_bank[h // 8]
                if n == 0:
                    for kt in range(QT):
                        ins = pe.matmul(dst[rows, col:col + SEQ], v[n][:, b * QT + kt, kh, :],
                                        p[:, kt * SEQ:(kt + 1) * SEQ], start=(kt == 0), stop=(kt == QT - 1))
                else:
                    pe.matmul(dst[rows, col + P:col + SEQ], v[n][:, b * QT + 1, kh, :], p[:, SEQ:SEQ + P],
                              start=True, stop=False, skip_group_check=True)
                    ins = pe.matmul(dst[rows, col:col + SEQ], v[n][:, b * QT, kh, :], p[:, 0:SEQ],
                                    start=False, stop=True, skip_group_check=True)
                ins.then_inc(pv_ready[n], 1)

            def turn_back(half, n, b):
                pe.wait_ge(pvs_ready[n], (half * HS + b + 1) * 2)
                for qt in range(QT):
                    r = ring_use(n, b, HEADS + qt)
                    wait_ring(half, n, r)
                    for grp in range(4):
                        ins = pe.transpose(st_bank[r % 3][:, grp * P:(grp + 1) * P],
                                           pvs[:, grp, qt * P:(qt + 1) * P], ident[:, :])
                    ins.then_inc(turned_back[n], 1)

            def attention(half, n):
                units = len(UNITS[n])
                pe.wait_ge(job_done[n], (half + 1) * JOBS[n])
                pe.wait_ge(stacked[n][0], (half + 1) * 12 * 16)
                for u in range(units):
                    unit(half, n, 0, u)
                turn_maxima(half, n, 0)
                for b in range(HS):
                    pe.wait_ge(neg_stacked[n], (half * HS + b + 1) * 32)
                    if b == 1:
                        pe.wait_ge(stacked[n][1], (half + 1) * 12 * 16)
                    for s in range(HEADS):
                        scores(half, n, b, s)
                        if b * HEADS + s >= LAG:
                            values(half, n, b * HEADS + s - LAG)
                        if b + 1 < HS:
                            for u in range(2 * s, min(2 * s + 2, units)):
                                unit(half, n, b + 1, u)
                        if b > 0 and s == TURN:
                            turn_back(half, n, b - 1)
                        if s == 11 and b + 1 < HS:
                            turn_maxima(half, n, b + 1)
                for i in range(HS * HEADS - LAG, HS * HEADS):
                    values(half, n, i)
                turn_back(half, n, HS - 1)

            def out_project(half):
                pe.wait_ge(rows_moved, half + 1)
                job = 0
                for c in range(CHUNKS):
                    for k in range(KD):
                        for t in range(CT):
                            ins = pe.transpose(bank[job][:, t * P:(t + 1) * P],
                                               xn[:, c * CT + t, k * P:(k + 1) * P], ident[:, :])
                        ins.then_inc(job_ready[1], 1)
                        job += 1
                pe.wait_ge(job_done[1], half * JOBS[1] + job)
                for i in range(HT // 2):
                    bank_free(half, 1, job, 0)
                    for t in range(2):
                        for k in range(KD):
                            ins = pe.matmul(bank[job % JOB_BANKS][:, t * D:(t + 1) * D],
                                            xnT[:, k, (2 * i + t) * P:(2 * i + t + 1) * P], wp[:, k, :],
                                            start=(k == 0), stop=(k == KD - 1))
                    ins.then_inc(job_ready[1], 1)
                    job += 1

            def select(half):
                job = JOB_F
                for c in range(CHUNKS):
                    for k in range(KD):
                        bank_free(half, 1, job, 0)
                        transposes(half, 1, job, 0, c, k)
                        job += 1
                pe.wait_ge(job_done[1], half * JOBS[1] + job)
                for i in range(HT // 2):
                    bank_free(half, 1, job, 0)
                    for t in range(2):
                        for k in range(KD):
                            ins = pe.matmul(bank[job % JOB_BANKS][:, t * FW:(t + 1) * FW],
                                            xnT[:, k, (2 * i + t) * P:(2 * i + t + 1) * P], wf[:, k, :],
                                            start=(k == 0), stop=(k == KD - 1))
                    ins.then_inc(job_ready[1], 1)
                    job += 1
                pe.wait_ge(selected, half + 1)
                for c in range(CHUNKS):
                    bank_free(half, 1, job, 0)
                    for t in range(CT):
                        ins = pe.transpose(bank[job % JOB_BANKS][0:MW, t * P:(t + 1) * P],
                                           mm[:, c * CT + t, :], ident[:, :])
                    ins.then_inc(job_ready[1], 1)
                    job += 1
                pe.wait_ge(job_done[1], half * JOBS[1] + job)
                for i in range(HT // 2):
                    bank_free(half, 1, job, 0)
                    for t in range(2):
                        ins = pe.matmul(bank[job % JOB_BANKS][:, t * D:(t + 1) * D],
                                        mT[:, (2 * i + t) * P:(2 * i + t + 1) * P], wd[:, :],
                                        start=True, stop=True)
                    ins.then_inc(job_ready[1], 1)
                    job += 1

            for half in range(HALVES):
                project(half, 0)
                attention(half, 0)
            pe.wait_ge(products_made, 1)
            for k in range(KD):
                mm_ = pe.matmul(bank[0][:, 0:FW], ones[:, :], prod[:, k, :], start=(k == 0), stop=(k == KD - 1))
            mm_.then_inc(sums_made, 1)
            pe.wait_ge(sums_copied, 1)
            for half in range(HALVES):
                out_project(half)
                select(half)
                project(half, 1)
                attention(half, 1)
            for n in range(TOKENS // CHUNK * KD):
                c, k = divmod(n, KD)
                pe.wait_ge(xn4_ready, (c + 1) * CT)
                if n >= 4:
                    pe.wait_ge(turn4_copied, n - 3)
                for t in range(CT):
                    ins = pe.transpose(bank[n % 4][:, t * P:(t + 1) * P],
                                       xn4[:, c * CT + t, k * P:(k + 1) * P], ident[:, :])
                ins.then_inc(turn4_ready, 1)
            pe.wait_ge(turn4_copied, TOKENS // CHUNK * KD)
            for t in range(TILES):
                for k in range(KD):
                    ins = pe.matmul(bank[6][:, t * EXPERTS:(t + 1) * EXPERTS], xnT4[:, k, t * P:(t + 1) * P],
                                    wr[:, k, :], start=(k == 0), stop=(k == KD - 1))
            ins.then_inc(logits_ready, 1)

            def ranks():
                pe.wait_ge(chosen_ready, 1)
                all_c = chosen[:, :, :].rearrange("p t e -> p (t e)")
                for t in range(1, TILES):
                    pe.matmul(bank[7][:, t * EXPERTS:te], onesb[:, :], all_c[:, 0:te - t * EXPERTS],
                              start=(t == 1), stop=False, skip_group_check=True)
                pe.matmul(bank[7][:, :], before[:, :], all_c, start=False, stop=True, skip_group_check=True)
                for t in range(TILES):
                    ins = pe.matmul(bank[5][:, 0:EXPERTS], onesb[:, :], chosen[:, t, :],
                                    start=(t == 0), stop=(t == TILES - 1))
                ins.then_inc(ranks_ready, 1)

            def shared_up(c):
                if c >= 1:
                    pe.wait_ge(sgu_clipped, c)
                for j in range(2):
                    for k in range(KD):
                        at0 = k * 2 * INNER + j * INNER
                        ins = pe.matmul(bank[j][:, :], wsh[:, at0:at0 + INNER],
                                        xnT4[:, k, c * CHUNK:(c + 1) * CHUNK], start=(k == 0), stop=(k == KD - 1))
                ins.then_inc(sgu_ready, 1)

            def shared_down(c):
                pe.wait_ge(shid_ready, c + 1)
                for j in range(2):
                    n = 2 * c + j
                    if n >= 2:
                        pe.wait_ge(sdown_added, n - 1)
                    for t in range(2):
                        at0 = (2 * j + t) * P
                        ins = pe.matmul(bank[2 + j][:, t * D:(t + 1) * D], sh[:, at0:at0 + P],
                                        wsh[:, 2 * KD * INNER:EW], start=True, stop=True)
                    ins.then_inc(sdown_ready, 1)

            ranks()
            for c in range(TOKENS // CHUNK):
                shared_up(c)
                shared_down(c)

            pe.wait_ge(experts_loaded, 16)
            pe.wait_ge(blocks_ready, 1)
            pe.wait_ge(sdown_added, TOKENS // CHUNK * 2)

            def turn_block(b, i, q, again):
                p = q % 2
                pe.wait_ge(xb_loaded[q], (i + 1) * 16)
                if again:
                    pe.wait_ge(xbT_copied, b - 1)
                for k in range(KD):
                    ins = pe.transpose(bank[p][:, k * P:(k + 1) * P], xb[:, q, k * P:(k + 1) * P], ident[:, :])
                ins.then_inc(xb_turned, 1)

            def expert_of(b):
                return pe.value_load(eb_i[0:1, bass.ds(b, 1)], min_val=0, max_val=EXPERTS - 1)

            def gate_up(b, p, again):
                pe.wait_ge(xbT_copied, b + 1)
                pe.wait_ge(staged, b + 1)
                if again:
                    pe.wait_ge(gu_clipped, b - 1)
                for g in range(2):
                    for k in range(KD):
                        ins = pe.matmul(bank[2 + p][:, g * P:(g + 1) * P],
                                        wgu[:, p, (k * 2 + g) * INNER:(k * 2 + g + 1) * INNER], xbT[:, p, k, :],
                                        start=(k == 0), stop=(k == KD - 1))
                ins.then_inc(gu_ready, 1)

            def down(b, p, again):
                e = expert_of(b)
                pe.wait_ge(hid_ready, b + 1)
                if again:
                    pe.wait_ge(yb_copied, b - 1)
                pe.matmul(bank[6 + p][:, 0:D], hid[:, p, :], arena[:, bass.ds(e * EW + 2 * KD * INNER, D)],
                          start=True, stop=True).then_inc(y_ready, 1)

            def pe_step(s, i, q, first=8):
                p = q % 2
                turn_block(s, i, q, first >= 2)
                if first >= 1:
                    gate_up(s - 1, 1 - p, first >= 3)
                if first >= 2:
                    down(s - 2, p, first >= 4)

            for s in range(8):
                pe_step(s, s // 4, s % 4, s)
            trips = block_trips(pe)
            with pe.Fori(2, trips) as i:
                for j in range(4):
                    pe_step(4 * i + j, i, j)
            end = trips * 4
            gate_up(end - 1, 1, True)
            down(end - 2, 0, True)
            down(end - 1, 1, True)

        @block.vector
        def _(dve):
            for qt in range(2):
                dve.memset(pv_bank[qt][:, :], 0.0).then_inc(constants_made, 1)
            dve.wait_ge(constants_made, CONSTANTS)

            steps = [0]

            def step(half, n, ins):
                steps[0] += 1
                ins.then_inc(dve_step[n], 1)
                dve.wait_ge(dve_step[n], half * DVE_STEPS[n] + steps[0])

            def norm(half, n, k):
                for t in range(HT):
                    ins = dve.bn_stats(st[:, t, :], x[:, half * HT + t, :])
                step(half, n, ins)
                for t in range(HT):
                    ins = dve.bn_aggr(mv[:, t, :], st[:, t, :])
                step(half, n, ins)
                dve.tensor_scalar(var[:, 0:HT], mv[:, 0:HT, 1], EPS, None, ALU.add).then_inc(var_ready[n], 1)
                dve.wait_ge(sd_ready[n], half * NORMS[n] + k + 1)
                step(half, n, dve.reciprocal(rstd[:, 0:HT], sd[:, 0:HT]))
                for t in range(HT):
                    dve.tensor_scalar(xn[:, t, :], x[:, half * HT + t, :], mv[:, t, 0:1], rstd[:, t:t + 1],
                                      ALU.subtract, ALU.mult).then_inc(xn_ready[n], 1)

            def turn_copy(half, n, job, c, k):
                dve.wait_ge(job_ready[n], half * JOBS[n] + job + 1)
                dve.tensor_copy(xnT[:, k, c * CHUNK:(c + 1) * CHUNK], bank[job % JOB_BANKS][:, :]
                                ).then_inc(job_done[n], 1)

            def project(half, n):
                kv = HEADS if n == 0 else GROUPS
                for i, (c, kind) in enumerate(LAYER_JOBS[n]):
                    job = JOB0[n] + i
                    b = bank[job % JOB_BANKS]
                    if kind[0] == "T":
                        turn_copy(half, n, job, c, int(kind[1]))
                    elif kind[0] in "QK":
                        j = SPLITS[n].index((c, kind))
                        slot = j % RING[n]
                        rows = GROUPS * HD if n == 1 and kind == "K0" else P
                        dve.wait_ge(hi_ready[n], half * len(SPLITS[n]) + j + 1)
                        if j >= RING[n]:
                            dve.wait_ge(low_ready[n], half * len(SPLITS[n]) + j - RING[n] + 1)
                        if n == 0:
                            ins = dve.tensor_tensor(rest[:, slot, :], b[:, :], parts[:, slot, 0, :], ALU.subtract)
                        else:
                            bias = bk[:, :] if kind == "K0" else bq[:, int(kind[1]):int(kind[1]) + 1]
                            ins = dve.scalar_tensor_tensor(out=rest[0:rows, slot, :], in0=b[0:rows, :], scalar=bias,
                                                           in1=parts[0:rows, slot, 0, :],
                                                           op0=ALU.add, op1=ALU.subtract)
                        ins.then_inc(job_done[n], 1)
                    else:
                        width = kv * HD
                        per = 512 // width if n == 0 else CT
                        dve.wait_ge(job_ready[n], half * JOBS[n] + job + 1)
                        tile = c * CT + int(kind[1]) * per
                        src = b[:, 0:per * width].rearrange("p (t h d) -> p t h d", t=per, d=HD)
                        for t in range(per):
                            if n == 0:
                                ins = dve.tensor_copy(v[0][:, tile + t, :, 0:HD], src[:, t])
                            else:
                                ins = dve.tensor_tensor(v[1][:, tile + t, :, 0:HD], src[:, t],
                                                        bvb[:, :].rearrange("p (h d) -> p h d", d=HD), ALU.add)
                        ins.then_inc(job_done[n], 1)

            def unit(half, n, b, u):
                qt, h0, nh, nk = UNITS[n][u]
                i = b * len(UNITS[n]) + u
                dve.wait_ge(unit_ready[n], half * HS * len(UNITS[n]) + i + 1)
                dve.tensor_reduce(mx[:, qt, h0:h0 + nh],
                                  unit_bank[i % 2][:, 0:nh * nk].rearrange("p (h k) -> p h k", h=nh),
                                  AX.X, ALU.max).then_inc(unit_done[n], 1)

            def minus_maxima(half, n, b):
                dve.wait_ge(unit_done[n], (half * HS + b + 1) * len(UNITS[n]))
                step(half, n, dve.tensor_scalar(neg[:, :, 0, :], mx[:, :, :], -1.0, None, ALU.mult))
                dve.scalar_tensor_tensor(out=neg[:, :, 1, :], in0=mx[:, :, :], scalar=-1.0, in1=neg[:, :, 0, :],
                                         op0=ALU.mult, op1=ALU.subtract).then_inc(neg_ready[n], 1)

            def divide(half, n, b):
                for qt in range(QT):
                    dve.wait_ge(turned_back[n], (half * HS + b) * QT + qt + 1)
                    pv = st_bank[ring_use(n, b, HEADS + qt) % 3][:, :].rearrange("p (h d) -> p h d", d=32)
                    step(half, n, dve.reciprocal(rec[:, qt, :], pv[:, :, HD]))
                    if n == 0:
                        for e in range(2):
                            heads = slice(e * SEQS, (e + 1) * SEQS)
                            ins = dve.tensor_tensor(ctx0[:, :, qt, half * 2 * HS + 2 * b + e, :],
                                                    pv[:, heads, 0:HD],
                                                    rec[:, qt, heads].unsqueeze(2).broadcast_to([P, SEQS, HD]),
                                                    ALU.mult)
                    else:
                        ins = dve.tensor_tensor(att[:, qt, :].rearrange("p (h d) -> p h d", d=HD), pv[:, :, 0:HD],
                                                rec[:, qt, :].unsqueeze(2).broadcast_to([P, HEADS, HD]), ALU.mult)
                    ins.then_inc(divided[n], 1)
                if n == 1:
                    dve.wait_ge(divided[1], (half * HS + b + 1) * QT)
                    xb_ = x[:, half * HT + b * QT:half * HT + (b + 1) * QT, :]
                    ins = dve.tensor_tensor(xb_, xb_, att[:, :, :], ALU.add)
                    if b == HS - 1:
                        step(half, n, ins)

            def attention(half, n):
                units = len(UNITS[n])
                for u in range(units):
                    unit(half, n, 0, u)
                minus_maxima(half, n, 0)
                for b in range(HS):
                    for s in range(HEADS):
                        if b > 0 and s == TURN + 1:
                            divide(half, n, b - 1)
                        if b + 1 < HS:
                            for u in range(2 * s, min(2 * s + 2, units)):
                                unit(half, n, b + 1, u)
                            if 2 * s + 2 == units:
                                minus_maxima(half, n, b + 1)
                divide(half, n, HS - 1)

            def add_pairs(half, job):
                for i in range(HT // 2):
                    dve.wait_ge(job_ready[1], half * JOBS[1] + job + 1)
                    xb = x[:, bass.ds(half * HT + 2 * i, 2), :]
                    dve.tensor_tensor(xb, xb, bank[job % JOB_BANKS][:, :].rearrange("p (t d) -> p t d", t=2),
                                      ALU.add).then_inc(job_done[1], 1)
                    job += 1
                dve.wait_ge(job_done[1], half * JOBS[1] + job)

            def out_project(half):
                dve.wait_ge(bias_added, HALVES)
                dve.wait_ge(divided[0], SEQS * QT)
                dve.tensor_copy(xn[:, :, :], ctx0[:, bass.ds(half * HS, HS), :, :, :]
                                .rearrange("p s q h d -> p (s q) (h d)")).then_inc(rows_moved, 1)
                for c in range(CHUNKS):
                    for k in range(KD):
                        turn_copy(half, 1, c * KD + k, c, k)
                add_pairs(half, CHUNKS * KD)

            def select(half):
                job = JOB_F
                for c in range(CHUNKS):
                    for k in range(KD):
                        turn_copy(half, 1, job, c, k)
                        job += 1
                for i in range(HT // 2):
                    dve.wait_ge(job_ready[1], half * JOBS[1] + job + 1)
                    dve.tensor_tensor(g[:, 2 * i:2 * i + 2, :],
                                      bank[job % JOB_BANKS][:, 0:2 * FW].rearrange("p (t f) -> p t f", t=2),
                                      constb[:, :].unsqueeze(1).broadcast_to([P, 2, FW]), ALU.subtract
                                      ).then_inc(job_done[1], 1)
                    job += 1
                dve.wait_ge(job_done[1], half * JOBS[1] + job)
                a = NSEL * SELW
                wide = [P, HT, NSEL]

                def row(t):
                    return t[:, :].unsqueeze(2).broadcast_to(wide)

                def col(t):
                    return t[:, :].unsqueeze(1).broadcast_to(wide)

                dve.wait_ge(squares_ready, (half + 1) * HT)
                dve.scalar_tensor_tensor(out=sc[2][:, :, :], in0=g[:, :, a:a + NSEL], scalar=-2.0, in1=row(xx),
                                         op0=ALU.mult, op1=ALU.add)
                step(half, 1, dve.tensor_tensor(sq[:, :, :], g[:, :, 0:a], g[:, :, 0:a], ALU.mult))
                dve.reciprocal(sc[3][:, :, :], sc[2][:, :, :])
                step(half, 1, dve.tensor_reduce(sc[0][:, :, :], sq[:, :, :].rearrange("p t (n s) -> p t n s", s=SELW),
                                             AX.X, ALU.add))
                step(half, 1, dve.tensor_tensor(sc[1][:, :, :], sc[0][:, :, :], sc[3][:, :, :], ALU.mult))
                step(half, 1, dve.tensor_tensor(sc[2][:, :, :], sc[1][:, :, :], col(cenb), ALU.subtract))
                step(half, 1, dve.tensor_tensor(sc[3][:, :, :], sc[2][:, :, :], col(slob), ALU.mult))
                dve.tensor_scalar(sc[0][:, :, :], sc[3][:, :, :], -80.0, None, ALU.max).then_inc(logit_ready, 1)
                dve.wait_ge(gate_exp_ready, half + 1)
                step(half, 1, dve.tensor_scalar(sc[2][:, :, :], sc[1][:, :, :], 1.0, None, ALU.add))
                step(half, 1, dve.reciprocal(sc[3][:, :, :], sc[2][:, :, :]))
                step(half, 1, dve.tensor_reduce(top[:, :], sc[3][:, :, :], AX.X, ALU.max))
                dve.tensor_scalar(keep[:, :], top[:, :], -1.0, 1.0, ALU.mult, ALU.add)
                step(half, 1, dve.tensor_tensor(sc[0][:, :, :], sc[3][:, :, :], row(top), ALU.is_equal))
                step(half, 1, dve.scalar_tensor_tensor(out=sc[1][:, :, :], in0=sc[0][:, :, :], scalar=-float(NSEL),
                                                    in1=col(iota8), op0=ALU.mult, op1=ALU.add))
                step(half, 1, dve.tensor_reduce(least[:, :], sc[1][:, :, :], AX.X, ALU.min))
                step(half, 1, dve.tensor_tensor(sc[2][:, :, :], sc[1][:, :, :], row(least), ALU.is_equal))
                step(half, 1, dve.tensor_tensor(mm[:, :, NSEL * LORA:MW], sc[2][:, :, :], row(top), ALU.mult))
                for t in range(HT):
                    dve.tensor_tensor(mm[:, t, 0:NSEL * LORA].rearrange("p (n h) -> p n h", h=LORA),
                                      g[:, t, a + NSEL:FW].rearrange("p (n h) -> p n h", h=LORA),
                                      mm[:, t, NSEL * LORA:MW].unsqueeze(2).broadcast_to([P, NSEL, LORA]), ALU.mult)
                    ins = dve.scalar_tensor_tensor(out=x[:, half * HT + t, :], in0=xn[:, t, :],
                                                   scalar=keep[:, t:t + 1], in1=x[:, half * HT + t, :],
                                                   op0=ALU.mult, op1=ALU.add)
                ins.then_inc(selected, 1)
                for c in range(CHUNKS):
                    dve.wait_ge(job_ready[1], half * JOBS[1] + job + 1)
                    dve.tensor_copy(mT[:, c * CHUNK:(c + 1) * CHUNK], bank[job % JOB_BANKS][0:MW, :]
                                    ).then_inc(job_done[1], 1)
                    job += 1
                dve.wait_ge(selected, half + 1)
                add_pairs(half, job)

            for half in range(HALVES):
                steps[0] = 0
                dve.wait_ge(x_loaded, (half + 1) * 16)
                norm(half, 0, 0)
                project(half, 0)
                attention(half, 0)
                assert steps[0] == DVE_STEPS[0], steps[0]
            dve.wait_ge(weights_loaded, 16 * len(WEIGHTS))
            sel_w = wf[:, :, 0:NSEL * SELW].rearrange("p k (n s) -> p k n s", s=SELW)
            dif_w = wf[:, :, NSEL * SELW:NSEL * SELW + NSEL]
            upd_w = wf[:, :, NSEL * SELW + NSEL:FW].rearrange("p k (n s) -> p k n s", s=LORA)
            for k in range(KD):
                dve.tensor_tensor(prod[:, k, 0:NSEL * SELW].rearrange("p (n s) -> p n s", s=SELW), sel_w[:, k],
                                  dif_w[:, k].unsqueeze(2).broadcast_to([P, NSEL, SELW]), ALU.mult)
                dve.scalar_tensor_tensor(out=prod[:, k, NSEL * SELW:NSEL * SELW + NSEL], in0=dif_w[:, k],
                                         scalar=0.5, in1=dif_w[:, k], op0=ALU.mult, op1=ALU.mult)
                ins = dve.tensor_tensor(prod[:, k, NSEL * SELW + NSEL:FW].rearrange("p (n s) -> p n s", s=LORA),
                                        upd_w[:, k], wdb[:, k].unsqueeze(2).broadcast_to([P, NSEL, LORA]), ALU.mult)
            ins.then_inc(products_made, 1)
            dve.wait_ge(sums_made, 1)
            dve.tensor_copy(constb[:, :], bank[0][:, 0:FW]).then_inc(sums_copied, 1)
            dve.wait_ge(sums_copied, 1)
            for half in range(HALVES):
                steps[0] = 0
                out_project(half)
                norm(half, 1, 0)
                select(half)
                norm(half, 1, 1)
                project(half, 1)
                attention(half, 1)
                assert steps[0] == DVE_STEPS[1], steps[0]
            moe_steps = [0]

            def then(ins):
                moe_steps[0] += 1
                ins.then_inc(moe_step, 1)
                dve.wait_ge(moe_step, moe_steps[0])

            for t in range(TILES):
                ins = dve.bn_stats(st[:, t, :], x[:, t, :])
            then(ins)
            for t in range(TILES):
                ins = dve.bn_aggr(mv[:, t, :], st[:, t, :])
            then(ins)
            dve.tensor_scalar(var[:, :], mv[:, :, 1], EPS, None, ALU.add).then_inc(var4_ready, 1)
            dve.wait_ge(sd4_ready, 1)
            then(dve.reciprocal(rstd[:, :], sd[:, :]))
            for t in range(TILES):
                dve.tensor_scalar(xn4[:, t, :], x[:, t, :], mv[:, t, 0:1], rstd[:, t:t + 1],
                                  ALU.subtract, ALU.mult).then_inc(xn4_ready, 1)
            for n in range(TOKENS // CHUNK * KD):
                c, k = divmod(n, KD)
                dve.wait_ge(turn4_ready, n + 1)
                dve.tensor_copy(xnT4[:, k, c * CHUNK:(c + 1) * CHUNK], bank[n % 4][:, :]).then_inc(turn4_copied, 1)

            dve.wait_ge(logits_ready, 1)
            then(dve.tensor_copy(lg, bank[6][:, :].rearrange("p (t e) -> p t e", t=TILES)))
            dve.scalar_tensor_tensor(out=sp1, in0=lg, scalar=-1.0, in1=lg, op0=ALU.mult, op1=ALU.min
                                     ).then_inc(route_ready, 1)
            dve.wait_ge(route_act, 1)
            dve.tensor_scalar(sbi, sbi, 1.0, None, ALU.add).then_inc(route_ready, 1)
            dve.wait_ge(route_act, 2)
            dve.scalar_tensor_tensor(out=sbi, in0=lg, scalar=0.0, in1=sp1, op0=ALU.max, op1=ALU.add
                                     ).then_inc(route_ready, 1)
            dve.wait_ge(route_act, 3)
            by_tile = [P, TILES, EXPERTS]
            by_pick = [P, TILES, TOPK, EXPERTS]
            then(dve.tensor_tensor(sbi, sco, ebb[:, :].unsqueeze(1).broadcast_to(by_tile), ALU.add))
            for t in range(TILES):
                ins = dve.max(m8[:, t, :], sbi[:, t, :])
            then(ins)
            for t in range(TILES):
                ins = dve.max_index(i8[:, t, :], m8[:, t, :], sbi[:, t, :])
            then(ins)
            then(dve.tensor_copy(pk[0][:, :, :], i8[:, :, 0:TOPK]))
            then(dve.tensor_tensor(pick[:, :, :, :],
                                   iota32[:, :].unsqueeze(1).unsqueeze(1).broadcast_to(by_pick),
                                   pk[0][:, :, :].unsqueeze(3).broadcast_to(by_pick), ALU.is_equal))
            with nc.allow_low_precision("sums of four zeros and ones"):
                dve.tensor_reduce(chosen[:, :, :], pick[:, :, :, :].rearrange("p t k e -> p t e k"),
                                  AX.X, ALU.add).then_inc(chosen_ready, 1)
            then(dve.tensor_tensor(work, pick[:, :, :, :], sco.unsqueeze(2).broadcast_to(by_pick), ALU.mult))
            then(dve.tensor_reduce(pk[0][:, :, :], work, AX.X, ALU.add))
            then(dve.tensor_reduce(ps[0][:, :], pk[0][:, :, :], AX.X, ALU.add))
            then(dve.tensor_scalar(ps[1][:, :], ps[0][:, :], 1e-20, None, ALU.add))
            then(dve.reciprocal(ps[0][:, :], ps[1][:, :]))
            then(dve.tensor_tensor(pk[1][:, :, :], pk[0][:, :, :],
                                   ps[0][:, :].unsqueeze(2).broadcast_to([P, TILES, TOPK]), ALU.mult))
            dve.wait_ge(ranks_ready, 1)
            then(dve.tensor_scalar(cnti[0][:, :], bank[5][:, 0:EXPERTS], float(P - 1), None, ALU.add))
            then(dve.tensor_scalar(cnti[1][:, :], cnti[0][:, :], P.bit_length() - 1, None, ALU.logical_shift_right))
            then(dve.tensor_copy(cnt[0][:, :], cnti[1][:, :]))
            ee = [P, EXPERTS, EXPERTS]
            pair = exps[:, 0:EXPERTS * EXPERTS].rearrange("p (e f) -> p e f", e=EXPERTS)
            then(dve.tensor_tensor(pair, iota32[:, :].unsqueeze(2).broadcast_to(ee),
                                   iota32[:, :].unsqueeze(1).broadcast_to(ee), ALU.is_gt))
            then(dve.tensor_tensor(pair, pair, cnt[0][:, :].unsqueeze(1).broadcast_to(ee), ALU.mult))
            then(dve.tensor_reduce(cnt[1][:, :], pair, AX.X, ALU.add))
            then(dve.tensor_tensor(cnt[2][:, :], cnt[0][:, :], cnt[1][:, :], ALU.add))
            then(dve.tensor_scalar(cnt[3][:, :], cnt[1][:, :], float(P), None, ALU.mult))
            then(dve.tensor_tensor(slots_e, bank[7][:, :].rearrange("p (t e) -> p t e", t=TILES),
                                   cnt[3][:, :].unsqueeze(1).broadcast_to(by_tile), ALU.add))
            then(dve.tensor_tensor(work, pick[:, :, :, :], slots_e.unsqueeze(2).broadcast_to(by_pick), ALU.mult))
            then(dve.tensor_reduce(pk[0][:, :, :], work, AX.X, ALU.add))
            dve.tensor_copy(slot[:, :, :], pk[0][:, :, :]).then_inc(slots_ready, 1)
            dve.wait_ge(pool_step, 6)
            half_b = BLOCKS // 2
            be = [1, half_b, EXPERTS]
            for i in range(2):
                rows = slice(i * half_b, (i + 1) * half_b)
                over = exps[0:1, 0:half_b * EXPERTS].rearrange("p (b e) -> p b e", b=half_b)
                then(dve.tensor_tensor(over, cnt[2][0:1, :].unsqueeze(1).broadcast_to(be),
                                       iota_b[:, rows].unsqueeze(2).broadcast_to(be), ALU.is_le))
                then(dve.tensor_reduce(eb_f[:, rows], over, AX.X, ALU.add))
            then(dve.tensor_scalar(trips_i[:, 0:1], cnt[2][0:1, EXPERTS - 1:EXPERTS], float(3 - 4 * FEWEST), None, ALU.add))
            then(dve.tensor_scalar(trips_i[:, 1:2], trips_i[:, 0:1], 2, None, ALU.logical_shift_right))
            dve.tensor_scalar(eb_i[:, :], eb_f[:, :], float(EXPERTS - 1), None, ALU.min).then_inc(blocks_ready, 1)

            for c in range(TOKENS // CHUNK):
                dve.wait_ge(sgu_ready, c + 1)
                if c:
                    dve.wait_ge(stanh_ready, c)
                dve.tensor_scalar(sg, bank[0][:, :], CLAMP, -CLAMP, ALU.min, ALU.max)
                dve.tensor_scalar(su, bank[1][:, :], CLAMP, -CLAMP, ALU.min, ALU.max).then_inc(sgu_clipped, 1)
                dve.wait_ge(sgu_clipped, c + 1)
                then(dve.scalar_tensor_tensor(out=su, in0=sg, scalar=0.5, in1=su, op0=ALU.mult, op1=ALU.mult))
                dve.wait_ge(stanh_ready, c + 1)
                dve.scalar_tensor_tensor(out=sh, in0=se, scalar=1.0, in1=su, op0=ALU.add, op1=ALU.mult
                                         ).then_inc(shid_ready, 1)
                for j in range(2):
                    dve.wait_ge(sdown_ready, 2 * c + j + 1)
                    xt = x[:, c * CT + 2 * j:c * CT + 2 * j + 2, :]
                    dve.tensor_tensor(xt, xt, bank[2 + j][:, :].rearrange("p (t d) -> p t d", t=2), ALU.add
                                      ).then_inc(sdown_added, 1)

            def clip(b, p):
                dve.wait_ge(gu_ready, b + 1)
                dve.tensor_scalar(gu[:, p, :, :].rearrange("p g i -> p (g i)"), bank[2 + p][:, 0:2 * INNER],
                                  CLAMP, -CLAMP, ALU.min, ALU.max).then_inc(gu_clipped, 1)

            def hidden(b, p, again):
                dve.wait_ge(gu_clipped, b + 1)
                dve.scalar_tensor_tensor(out=gu[:, p, 1, :], in0=gu[:, p, 0, :], scalar=0.5, in1=gu[:, p, 1, :],
                                         op0=ALU.mult, op1=ALU.mult).then_inc(hid_step, 1)
                dve.wait_ge(hid_step, b + 1)
                dve.wait_ge(ge_ready, b + 1)
                if again:
                    dve.wait_ge(y_ready, b - 1)
                dve.scalar_tensor_tensor(out=hid[:, p, :], in0=ge[:, p, :], scalar=1.0, in1=gu[:, p, 1, :],
                                         op0=ALU.add, op1=ALU.mult).then_inc(hid_ready, 1)

            def stage(b, p):
                e = dve.value_load(eb_i[0:1, bass.ds(b, 1)], min_val=0, max_val=EXPERTS - 1)
                dve.tensor_copy(wgu[:, p, :], arena[:, bass.ds(e * EW, 2 * KD * INNER)]).then_inc(staged, 1)

            def dve_step_moe(s, p, first=8):
                if first < 9:
                    stage(s, p)
                clip(s - 1, 1 - p)
                hidden(s - 1, 1 - p, first >= 3)

            dve.wait_ge(experts_loaded, 16)
            dve.wait_ge(blocks_ready, 1)
            stage(0, 0)
            for s in range(1, 8):
                dve_step_moe(s, s % 2, s)
            trips = block_trips(dve)
            with dve.Fori(2, trips) as i:
                for j in range(4):
                    dve_step_moe(4 * i + j, j % 2)
            end = trips * 4
            dve_step_moe(end, 0, 9)
            for p in range(2):
                dve.wait_ge(y_stored[p], trips * 32)
                dve.tensor_copy(hold[:, p:p + 1], zero[0:1, 0:1]).then_inc(all_stored, 1)

            for n in range(TILES * TOPK):
                t, k = divmod(n, TOPK)
                dve.wait_ge(gathered[n % YG], (n // YG + 1) * 16)
                if k:
                    dve.wait_ge(y_added, n)
                dve.scalar_tensor_tensor(out=x[:, t, :], in0=yg[:, n % YG, :], scalar=pk[1][:, t, k:k + 1],
                                         in1=x[:, t, :], op0=ALU.mult, op1=ALU.add).then_inc(y_added, 1)


_SHAPES = "inputs as laid out below"


def _layout(i):
    a = {n: np.asarray(v) for n, v in i.items()}
    qkv = a["L0_attn_Wqkv"].reshape(HEADS, 3, HD, D).transpose(3, 1, 0, 2).reshape(D, 3 * D)

    def flat(w):
        return w.transpose(1, 0, 2).reshape(w.shape[1], -1)

    ffn = np.concatenate([flat(a["L0_ffn_select_weight"]), a["L0_ffn_select_mean_diff"].T,
                          flat(a["L0_ffn_lora_update"])], axis=1)
    down = np.concatenate([a["L0_ffn_lora_degen"].transpose(0, 2, 1).reshape(NSEL * LORA, D), a["L0_ffn_bias_w"]])
    qkv1 = np.concatenate([flat(a["L1_attn_Wq"]), flat(a["L1_attn_Wk"]), flat(a["L1_attn_Wv"])], axis=1)

    def halves(w):
        return w.reshape(w.shape[0], INNER, KD, P).transpose(0, 3, 2, 1)

    gate = np.concatenate([a["L1_ffn_gate_w"], a["L1_ffn_shared_gate_w"][None]])
    up = np.concatenate([a["L1_ffn_up_w"], a["L1_ffn_shared_up_w"][None]])
    dn = np.concatenate([a["L1_ffn_down_w"], a["L1_ffn_shared_down_w"][None]])
    gu = np.concatenate([halves(gate), halves(up)], axis=3).reshape(EXPERTS + 1, P, 2 * KD * INNER)
    experts = np.concatenate([gu, dn.transpose(0, 2, 1)], axis=2).transpose(1, 0, 2)
    return [a["L0_attn_query"].reshape(TOKENS, D), qkv, a["L0_attn_Wproj"].T, a["L0_attn_bproj"].reshape(1, D),
            ffn, a["L0_ffn_debias_w"].T, down, a["L0_ffn_imp_center"].reshape(1, NSEL),
            a["L0_ffn_imp_slope"].reshape(1, NSEL), qkv1, a["L1_attn_bq"].reshape(KD, P).T,
            a["L1_attn_bk"].reshape(GROUPS * HD, 1), a["L1_attn_bv"].reshape(1, GROUPS * HD),
            a["L1_ffn_router_w"].T, a["L1_ffn_expert_bias"].reshape(1, EXPERTS), experts]


def kernel(**inputs):
    import concourse.bacc as bacc
    from concourse.bass_utils import run_bass_kernel_spmd

    nc = bacc.Bacc("TRN2", target_bir_lowering=False, num_devices=1)
    arrays, args = {}, []
    for n, a in enumerate(_layout(inputs)):
        a = np.ascontiguousarray(a)
        arrays[f"in_{n}"] = a
        args.append(nc.dram_tensor(f"in_{n}", a.shape, mybir.dt.from_np(a.dtype), kind="ExternalInput").ap())
    args.append(nc.dram_tensor("out", (TOKENS, D), F32, kind="ExternalOutput").ap())
    nc.disable_value_cache = True
    two_block_kernel(nc, *args)
    r = run_bass_kernel_spmd(nc, [arrays], core_ids=[0])
    return r.results[0]["out"].reshape(SEQS, SEQ, D)
```
